# Optimizing a Trainium2 kernel written in Bass

```python
import numpy as np
import jax
import jax.numpy as jnp

def _softmax(x, axis=-1):
    return jax.nn.softmax(x, axis=axis)
def _gelu(x):
    return jax.nn.gelu(x, approximate=True)
def _silu(x):
    return jax.nn.silu(x)
def _sigmoid(x):
    return jax.nn.sigmoid(x)
def _layernorm(x, axis=-1, eps=1e-5):
    m = jnp.mean(x, axis=axis, keepdims=True)
    v = jnp.var(x, axis=axis, keepdims=True)
    return (x - m) / jnp.sqrt(v + eps)
def _scatter_add(tgt, idx, src, axis=0):
    return tgt.at[idx].add(src)
def _segment_sum(src, seg, n):
    return jax.ops.segment_sum(src, seg, n)

kernel_name = 'mk_conv_seq_d2_conv_nchw256_8379a1'

def setup_inputs(seed: int = 0):
    np.random.seed(seed)
    _w = jnp.asarray
    def _rec_inputs():
        import jax
        import jax.numpy as jnp
        _gk = jax.random.key(seed)
        x = -0.0002928 + 1 * jax.random.normal(jax.random.fold_in(_gk, 1), (4, 256, 64, 64), jnp.float32)
        return x
    x = _rec_inputs()
    def _L0_conv_setup():
        import jax, jax.numpy as jnp
        import numpy as np
        from jax import lax
        B, C, H, W = (4, 256, 64, 64)
        DN = ('NCHW', 'OIHW', 'NCHW')
        key = jax.random.key(seed)
        k1, k2, k3, k4, k5 = jax.random.split(key, 5)
        x = jax.random.normal(k1, (B, C, H, W), dtype=jnp.float32)
        w1 = jax.random.normal(k2, (128, C, 7, 7), dtype=jnp.float32) * 0.02
        b1 = jax.random.normal(k3, (128,), dtype=jnp.float32) * 0.02
        w2 = jax.random.normal(k4, (49, 128, 1, 1), dtype=jnp.float32) * 0.02
        b2 = jax.random.normal(k5, (49,), dtype=jnp.float32) * 0.02
        return {'x': x, 'w1': w1, 'b1': b1, 'w2': w2, 'b2': b2}
    _L0_conv_all = _L0_conv_setup()
    _L0_conv_in = {k: v for k, v in _L0_conv_all.items() if k in ('w1', 'b1', 'w2', 'b2', )}
    del _L0_conv_all

    def _L1_conv_setup():
        import jax, jax.numpy as jnp
        import numpy as np
        LN_EPS = 1e-05
        key = jax.random.key(seed)
        k0, k1, k2, k3, k4 = jax.random.split(key, 5)
        B_, F_, H_, T_ = (8, 256, 64, 512)
        S = 32
        x = jax.random.normal(k0, (B_, F_, H_, T_), dtype=jnp.float32)
        A = 0.1 * jax.random.normal(k1, (S, S), dtype=jnp.float32)
        Bvec = 0.1 * jax.random.normal(k2, (S,), dtype=jnp.float32)
        Cmat = 0.1 * jax.random.normal(k3, (S, F_), dtype=jnp.float32)
        D = 0.1 * jax.random.normal(k4, (F_,), dtype=jnp.float32)
        ln_w = jnp.ones((F_,), dtype=jnp.float32)
        ln_b = jnp.zeros((F_,), dtype=jnp.float32)
        return {'x': x, 'A': A, 'Bvec': Bvec, 'Cmat': Cmat, 'D': D, 'ln_w': ln_w, 'ln_b': ln_b}
    _L1_conv_all = _L1_conv_setup()
    _L1_conv_in = {k: v for k, v in _L1_conv_all.items() if k in ('A', 'Bvec', 'Cmat', 'D', 'ln_w', 'ln_b', )}
    del _L1_conv_all

    return {
        "x": x,
        "L0_conv_w1": _L0_conv_in["w1"],
        "L0_conv_b1": _L0_conv_in["b1"],
        "L0_conv_w2": _L0_conv_in["w2"],
        "L0_conv_b2": _L0_conv_in["b2"],
        "L1_conv_A": _L1_conv_in["A"],
        "L1_conv_Bvec": _L1_conv_in["Bvec"],
        "L1_conv_Cmat": _L1_conv_in["Cmat"],
        "L1_conv_D": _L1_conv_in["D"],
        "L1_conv_ln_w": _L1_conv_in["ln_w"],
        "L1_conv_ln_b": _L1_conv_in["ln_b"],
    }

def reference(x, L0_conv_w1, L0_conv_b1, L0_conv_w2, L0_conv_b2, L1_conv_A, L1_conv_Bvec, L1_conv_Cmat, L1_conv_D, L1_conv_ln_w, L1_conv_ln_b):
    import jax
    import jax.numpy as jnp
    def _L0_conv_ref(x, w1, b1, w2, b2):
        import jax, jax.numpy as jnp
        import numpy as np
        from jax import lax
        B, C, H, W = (4, 256, 64, 64)
        DN = ('NCHW', 'OIHW', 'NCHW')
        k = lax.conv_general_dilated(x, w1, window_strides=(1, 1), padding=[(6, 6), (6, 6)], rhs_dilation=(2, 2), dimension_numbers=DN) + b1[None, :, None, None]
        k = lax.conv_general_dilated(k, w2, window_strides=(1, 1), padding=[(0, 0), (0, 0)], dimension_numbers=DN) + b2[None, :, None, None]
        attn = jax.nn.softmax(k, axis=1)
        xp = jnp.pad(x, ((0, 0), (0, 0), (6, 6), (6, 6)))
        shifts = jnp.stack([xp[:, :, 2 * u:2 * u + x.shape[2], 2 * v:2 * v + x.shape[3]] for u in range(7) for v in range(7)], axis=1)
        return jnp.einsum('bkchw,bkhw->bchw', shifts, attn)

    def _L1_conv_ref(x, A, Bvec, Cmat, D, ln_w, ln_b):
        import jax, jax.numpy as jnp
        import numpy as np
        LN_EPS = 1e-05
        T = x.shape[-1]
        s0 = jnp.zeros((A.shape[0],), dtype=x.dtype)

        def step(s, _):
            s = A @ s + Bvec
            return (s, s)
        _, states = jax.lax.scan(step, s0, None, length=T)
        yc = states @ Cmat
        y = jax.nn.gelu(yc.T[None, :, None, :] + x * D[None, :, None, None], approximate=False)
        out = x + y
        o = jnp.moveaxis(out, 1, -1)
        mu = jnp.mean(o, axis=-1, keepdims=True)
        var = jnp.var(o, axis=-1, keepdims=True)
        o = (o - mu) * jax.lax.rsqrt(var + LN_EPS) * ln_w + ln_b
        return jnp.moveaxis(o, -1, 1)

    def _gn(v, G=32, eps=1e-5):
        B_, C_, H_, W_ = v.shape
        g = v.reshape(B_, G, C_ // G, H_, W_)
        m = jnp.mean(g, axis=(2, 3, 4), keepdims=True)
        s = jnp.var(g, axis=(2, 3, 4), keepdims=True)
        return ((g - m) / jnp.sqrt(s + eps)).reshape(v.shape)

    def _ln_c(v, eps=1e-6):
        m = jnp.mean(v, axis=1, keepdims=True)
        s = jnp.var(v, axis=1, keepdims=True)
        return (v - m) / jnp.sqrt(s + eps)

    def _ln_t(v, eps=1e-5):
        m = jnp.mean(v, axis=-1, keepdims=True)
        s = jnp.var(v, axis=-1, keepdims=True)
        return (v - m) / jnp.sqrt(s + eps)

    def _to_tokens(v):
        B_, C_, H_, W_ = v.shape
        return v.reshape(B_, C_, H_ * W_).transpose(0, 2, 1)
    def _from_tokens(t, like):
        B_, C_, H_, W_ = like.shape
        return t.transpose(0, 2, 1).reshape(B_, C_, H_, W_)

    x = _L0_conv_ref(x, L0_conv_w1, L0_conv_b1, L0_conv_w2, L0_conv_b2)
    x = _L1_conv_ref(x, L1_conv_A, L1_conv_Bvec, L1_conv_Cmat, L1_conv_D, L1_conv_ln_w, L1_conv_ln_b)
    return x


_drawn_inputs = setup_inputs


def setup_inputs(seed=0):
    import zlib

    import numpy as np

    out = dict(_drawn_inputs(seed))
    spreads = {'L1_conv_ln_w': (1.0, 0.2), 'L1_conv_ln_b': (0.0, 0.1)}
    factors = {'L0_conv_b1': 8.0, 'L0_conv_b2': 3.067}
    for name, (base, spread) in spreads.items():
        noise = np.random.default_rng([zlib.crc32(name.encode()), seed]).standard_normal(out[name].shape)
        drawn = base * np.exp(spread * noise) if base else spread * noise
        out[name] = jnp.asarray(drawn.astype(out[name].dtype))
    for name, factor in factors.items():
        out[name] = (out[name] * factor).astype(out[name].dtype)
    return out
```

```python
from contextlib import ExitStack

import concourse.bass as bass
from concourse import mybir

F32 = mybir.dt.float32
F16 = mybir.dt.float16
U32 = mybir.dt.uint32
ALU = mybir.AluOpType
ACT = mybir.ActivationFunctionType
AX = mybir.AxisListType.X
ABSMAX = bass.bass_isa.ReduceOp.absmax

P = 128
BATCH, CH, HEIGHT, WIDTH = 4, 256, 64, 64
HALVES = CH // P
MID = 128
K7 = 7
TAPS = K7 * K7
ROWS, COLS = HEIGHT // 2, WIDTH // 2
PAD = 3
PROWS, PCOLS = ROWS + 2 * PAD, COLS + 2 * PAD
TILE_ROWS = ROWS // 2
VROWS = TILE_ROWS + 2
UNITS = BATCH * 2
STREAMS = 4 * 2 * K7 + K7
DIRECT = 4 * 2 * K7
TILES = 2 * (ROWS // 4)
BROWS = 4 + 2 * PAD
BANK = 512
LO = 64
STATE = 32
LN_EPS = 1e-5
SEL_TAPS = ((0, 7), (3, 7), (2, 7), (1, 7), (0, 6), (0, 5), (0, 4))
SEL_AT = PAD * COLS + COLS - 1 - PAD
ATT_SCALE = 4096.0
TRANSFORM = (0, 3, 1, 2)
PHASE_STEPS = (42, 42, 28, 28)
PHASE_START = (0, 42, 84, 112)
ROW_PAIRS = {0: (0, 2, ALU.subtract), 1: (1, 2, ALU.add), 2: (2, 1, ALU.subtract), 3: (3, 1, ALU.subtract)}


def prepare_weights(nc, sb, sem, C, w1, b1, w2, b2, A, Bvec, Cmat, D, ln_w, ln_b, x):
    with ExitStack() as ctx:
        def tmp(name, shape, dt=F32):
            return ctx.enter_context(nc.sbuf_tensor(name, shape, dt))

        w1raw = tmp("w1raw", [P, HALVES, P * TAPS])
        wc = tmp("wc", [P, HALVES, K7, K7 * TAPS])
        w2raw = tmp("w2raw", [TAPS, MID])
        w2t = tmp("w2t", [MID, TAPS])
        b1col = tmp("b1col", [MID, 1])
        b2col = tmp("b2col", [P, 1])
        ut = tmp("ut", [P, 2, 3, 2, K7 * TAPS])
        wmax = tmp("wmax", [P, 4])
        wall = tmp("wall", [P, 1])
        wsc = tmp("wsc", [P, 6])
        powA = tmp("powA", [STATE, 2, 2, STATE])
        states = tmp("states", [STATE, WIDTH])
        cm = tmp("cm", [STATE, CH])
        pw_ = ctx.enter_context(nc.psum_tensor("pw_", [P, 4, BANK], F32))
        pst = ctx.enter_context(nc.psum_tensor("pst", [P, 2, BANK], F32))
        s_w1 = sem("w1_in")
        s_w2 = sem("w2_in")
        s_small = sem("small_in")
        s_ident = sem("ident_set")
        s_g = sem("select_set")
        s_zero = sem("zeroed")
        s_w2t = sem("w2t_ready")
        s_w2s = sem("w2t_copied")
        s_comp = sem("composite_ready")
        s_wcp = sem("composite_copied")
        s_wmax = sem("wmax_made")
        s_wall = sem("wmax_all")
        s_wscale = sem("wscale_steps")
        s_u = sem("row_transform_steps")
        s_whi = sem("w_high_made")
        s_bias = sem("bias_summed")
        s_done = sem("weights_done")
        s_at = sem("a_transposed")
        s_pow = sem("powers_ready")
        s_powc = sem("powers_copied")
        s_yc = sem("yc_ready")

        w1v = w1.rearrange("m (h c) a b -> h m (c a b)", h=HALVES)
        with nc.Block() as block:
            @block.sync
            def _(sp):
                sp.dma_start(w2raw[:, :], w2.rearrange("k m a b -> k (m a b)")).then_inc(s_w2, 16)
                sp.dma_start(powA[:, 0, 0, :], A).then_inc(s_small, 16)
                sp.dma_start(w1raw[:, 0, :], w1v[0]).then_inc(s_w1, 16)
                sp.dma_start(w1raw[:, 1, :], w1v[1]).then_inc(s_w1, 16)
                for h in range(HALVES):
                    sp.dma_start(C["raw"][:, 0, h, PAD:PAD + ROWS, :], C["xrows"](0, 0, h)).then_inc(C["raw_in"][0], 16)

            @block.scalar
            def _(act):
                col = lambda a: a.rearrange("(p o) -> p o", o=1)
                act.dma_start(states[:, 0:1], col(Bvec)).then_inc(s_small, 16)
                act.dma_start(cm[:, :], Cmat).then_inc(s_small, 16)
                act.dma_start(b1col[:, :], col(b1)).then_inc(s_small, 16)
                act.wait_ge(s_zero, 1)
                act.dma_start(b2col[0:TAPS, :], col(b2)).then_inc(s_small, 16)
                act.dma_start(b2col[LO:LO + TAPS, :], col(b2)).then_inc(s_small, 16)
                for dst, src in ((C["dcol"], D), (C["lnw"], ln_w), (C["lnb"], ln_b)):
                    for h in range(HALVES):
                        act.dma_start(dst[:, h:h + 1], col(src[h * P:(h + 1) * P])).then_inc(s_small, 16)
                act.wait_ge(s_wscale, 6)
                for h in range(HALVES):
                    act.wait_ge(s_u, 3 * h + 3)
                    for i, (src, half) in enumerate(((wc[:, h, 0:5:4, :], 0), (ut[:, h, 1], 1),
                                                     (ut[:, h, 2], 1), (wc[:, h, 2:7:4, :], 0))):
                        nc.scalar.activation(
                            C["W"][:, 0, h, 14 * i:14 * i + 14, :].rearrange("p (s v) k -> p s (v k)", s=2),
                            src, ACT.Identity, scale=wsc[:, 3 + half:4 + half]).then_inc(s_whi, 1)
                    nc.scalar.activation(C["W"][:, 0, h, DIRECT:STREAMS, :].rearrange("p v k -> p (v k)"),
                                         wc[:, h, 3, :], ACT.Identity, scale=wsc[:, 3:4]).then_inc(s_whi, 1)

            @block.gpsimd
            def _(pool):
                for n, t in enumerate((C["id32"], C["id16"])):
                    nc.gpsimd.memset(t[:, :], 0.0).then_inc(s_ident, 1)
                    pool.wait_ge(s_ident, 2 * n + 1)
                    nc.gpsimd.affine_select(out=t[:, :], in_=t[:, :], compare_op=ALU.not_equal, fill=1.0, base=0,
                                            pattern=[[-1, P]], channel_multiplier=1).then_inc(s_ident, 1)
                nc.gpsimd.memset(C["sel"][:, :, :], 0.0).then_inc(s_g, 1)
                for n, base in enumerate((0, -LO)):
                    pool.wait_ge(s_g, 7 * n + 1)
                    for s, (v0, v1) in enumerate(SEL_TAPS):
                        v = C["sel"][:, s, SEL_AT:SEL_AT + K7 * COLS].rearrange("p (u c) -> p u c", u=K7)[:, :, v0:v1]
                        nc.gpsimd.affine_select(out=v, in_=v, compare_op=ALU.not_equal, fill=1.0, base=base - v0,
                                                pattern=[[-K7, K7], [-1, v1 - v0]],
                                                channel_multiplier=1).then_inc(s_g, 1)
                nc.gpsimd.memset(C["ones"][:, :], 1.0 / CH).then_inc(s_g, 1)
                nc.gpsimd.memset(C["eps"][:, :], LN_EPS).then_inc(s_g, 1)
                for t in (C["raw"][:, :, :, 0:PAD, :], C["raw"][:, :, :, PAD + ROWS:, :]):
                    for slot in range(2):
                        nc.gpsimd.memset(t[:, slot], 0.0).then_inc(s_g, 1)
                pool.wait_ge(s_wmax, 2)
                nc.gpsimd.partition_all_reduce(wall[:, :], wmax[:, 2:3], P, ABSMAX).then_inc(s_wall, 1)
                pool.wait_ge(s_g, 21)

            @block.tensor
            def _(pe):
                pe.wait_ge(s_ident, 2)
                pe.wait_ge(s_w2, 16)
                pe.transpose(pst[:, 0, 0:TAPS], w2raw[:, :], C["id32"][0:TAPS, 0:TAPS]).then_inc(s_w2t, 1)
                pe.wait_ge(s_small, 16 * 12)
                pe.wait_ge(s_w2s, 1)
                pe.transpose(pst[0:STATE, 0, 0:STATE], powA[:, 0, 0, :],
                             C["id32"][0:STATE, 0:STATE]).then_inc(s_at, 1)
                for j in range(6):
                    n = 1 << j
                    pe.wait_ge(s_powc, 3 * j + 1)
                    pe.matmul(pst[0:STATE, 0, 0:n], powA[:, j % 2, 1, :], states[:, 0:n], start=True, stop=True)
                    pe.matmul(pst[0:STATE, 0, 64:96], powA[:, j % 2, 1, :], powA[:, j % 2, 0, :],
                              start=True, stop=True)
                    pe.matmul(pst[0:STATE, 0, 128:160], powA[:, j % 2, 0, :], powA[:, j % 2, 1, :],
                              start=True, stop=True).then_inc(s_pow, 1)
                pe.wait_ge(s_powc, 19)
                for h in range(HALVES):
                    last = pe.matmul(pst[:, 0, h * WIDTH:(h + 1) * WIDTH], cm[:, h * P:(h + 1) * P], states[:, :],
                                     start=True, stop=True)
                last.then_inc(s_yc, 1)
                pe.matmul(pst[0:TAPS, 1, 0:1], w2t[:, :], b1col[:, :], start=True, stop=True)
                pe.matmul(pst[LO:LO + TAPS, 1, 0:1], w2t[:, :], b1col[:, :], start=True, stop=True).then_inc(s_bias, 1)
                for h in range(HALVES):
                    pe.wait_ge(s_w1, 16 * HALVES)
                    w1h = w1raw[:, h, :].rearrange("m (c t) -> m t c", t=TAPS)
                    for u in range(K7):
                        g = h * K7 + u
                        if g >= 4:
                            pe.wait_ge(s_wcp, g - 3)
                        for v in range(K7):
                            last = pe.matmul(pw_[:, g % 4, v * TAPS:(v + 1) * TAPS], w1h[:, u * K7 + v, :],
                                             w2t[:, :], start=True, stop=True)
                        last.then_inc(s_comp, 1)

            @block.vector
            def _(dve):
                nc.vector.memset(b2col[:, :], 0.0).then_inc(s_zero, 1)
                for t in (C["V"][:, 0, 0], C["V"][:, 0, 1], C["V"][:, 1, 0], C["V"][:, 1, 1]):
                    nc.vector.memset(t.rearrange("p h w r c -> p (h w r c)").bitcast(U32), 0).then_inc(s_zero, 1)
                nc.vector.memset(C["X"][:].rearrange("p l h w r c -> p (l h w r c)").bitcast(U32), 0).then_inc(s_zero, 1)
                nc.vector.memset(C["HL"][:].rearrange("p i k -> p (i k)").bitcast(U32), 0).then_inc(s_zero, 1)
                nc.vector.memset(C["AT"][:].rearrange("p w r c -> p (w r c)").bitcast(U32), 0).then_inc(s_zero, 1)
                dve.wait_ge(s_w2t, 1)
                nc.vector.tensor_copy(w2t[:, :], pst[:, 0, 0:TAPS]).then_inc(s_w2s, 1)
                dve.wait_ge(s_at, 1)
                nc.vector.tensor_copy(powA[:, 0, 1, :], pst[0:STATE, 0, 0:STATE]).then_inc(s_powc, 1)
                for j in range(6):
                    n = 1 << j
                    dve.wait_ge(s_pow, j + 1)
                    nc.vector.tensor_scalar(states[:, n:2 * n], pst[0:STATE, 0, 0:n], states[:, n - 1:n], None,
                                            ALU.add).then_inc(s_powc, 1)
                    nc.vector.tensor_copy(powA[:, (j + 1) % 2, 0, :], pst[0:STATE, 0, 64:96]).then_inc(s_powc, 1)
                    nc.vector.tensor_copy(powA[:, (j + 1) % 2, 1, :], pst[0:STATE, 0, 128:160]).then_inc(s_powc, 1)
                    dve.wait_ge(s_powc, 3 * j + 4)
                dve.wait_ge(s_yc, 1)
                nc.vector.tensor_copy(C["yc"][:, :, :], pst[:, 0, 0:HALVES * WIDTH].rearrange(
                    "p (h w) -> p h w", h=HALVES)).then_inc(s_done, 1)
                dve.wait_ge(s_bias, 1)
                dve.wait_ge(s_small, 16 * 12)
                nc.vector.tensor_copy(C["bias"][:, :], b2col[:, :]).then_inc(s_done, 1)
                dve.wait_ge(s_done, 2)
                for p0 in (0, LO):
                    nc.vector.tensor_tensor(C["bias"][p0:p0 + TAPS, :], b2col[p0:p0 + TAPS, :],
                                            pst[p0:p0 + TAPS, 1, 0:1], ALU.add).then_inc(s_done, 1)
                for g in range(HALVES * K7):
                    dve.wait_ge(s_comp, g + 1)
                    nc.vector.tensor_copy(wc[:, g // K7, g % K7, :], pw_[:, g % 4, 0:K7 * TAPS]).then_inc(s_wcp, 1)
                dve.wait_ge(s_wcp, HALVES * K7)
                nc.vector.tensor_reduce(wmax[:, 2:3], wc[:].rearrange("p h u t -> p (h u t)"), AX, ALU.max,
                                        apply_absolute_value=True).then_inc(s_wmax, 2)
                for h in range(HALVES):
                    nc.vector.tensor_tensor(ut[:, h, 0], wc[:, h, 0:5:4, :], wc[:, h, 2:7:4, :],
                                            ALU.add).then_inc(s_u, 1)
                    dve.wait_ge(s_u, 3 * h + 1)
                    nc.vector.tensor_tensor(ut[:, h, 1], ut[:, h, 0], wc[:, h, 1:6:4, :], ALU.add).then_inc(s_u, 1)
                    nc.vector.tensor_tensor(ut[:, h, 2], ut[:, h, 0], wc[:, h, 1:6:4, :], ALU.subtract).then_inc(s_u, 1)
                dve.wait_ge(s_wall, 1)
                nc.vector.tensor_scalar(wsc[:, 0:1], wall[:, :], 1e-30, None, ALU.max).then_inc(s_wscale, 1)
                dve.wait_ge(s_wscale, 1)
                nc.vector.tensor_scalar(wsc[:, 1:2].bitcast(U32), wsc[:, 0:1].bitcast(U32), 0x7F800000, None,
                                        ALU.bitwise_and).then_inc(s_wscale, 1)
                dve.wait_ge(s_wscale, 2)
                nc.vector.reciprocal(wsc[:, 2:3], wsc[:, 1:2]).then_inc(s_wscale, 1)
                dve.wait_ge(s_wscale, 3)
                nc.vector.tensor_scalar(wsc[:, 3:4], wsc[:, 2:3], 2.0 ** 13, None, ALU.mult).then_inc(s_wscale, 1)
                nc.vector.tensor_scalar(wsc[:, 4:5], wsc[:, 2:3], 2.0 ** 12, None, ALU.mult).then_inc(s_wscale, 1)
                nc.vector.tensor_scalar(C["winv"][:, :], wsc[:, 1:2], 2.0 ** -13, None, ALU.mult).then_inc(s_wscale, 1)
                dve.wait_ge(s_wscale, 6)
                for h in range(HALVES):
                    for i, (src, half) in enumerate(((wc[:, h, 0:5:4, :], 0), (ut[:, h, 1], 1),
                                                     (ut[:, h, 2], 1), (wc[:, h, 2:7:4, :], 0))):
                        dve.wait_ge(s_whi, 5 * h + i + 1)
                        hi, lo = (C["W"][:, l, h, 14 * i:14 * i + 14, :].rearrange("p (s v) k -> p s (v k)", s=2)
                                  for l in range(2))
                        nc.vector.scalar_tensor_tensor(out=lo, in0=src, scalar=wsc[:, 3 + half:4 + half], in1=hi,
                                                       op0=ALU.mult, op1=ALU.subtract).then_inc(s_done, 1)
                    dve.wait_ge(s_whi, 5 * h + 5)
                    hi, lo = (C["W"][:, l, h, DIRECT:STREAMS, :].rearrange("p v k -> p (v k)") for l in range(2))
                    nc.vector.scalar_tensor_tensor(out=lo, in0=wc[:, h, 3, :], scalar=wsc[:, 3:4], in1=hi,
                                                   op0=ALU.mult, op1=ALU.subtract).then_inc(s_done, 1)
                dve.wait_ge(s_done, 4 + 5 * HALVES)
                dve.wait_ge(s_zero, 8)


def conv_seq_kernel(nc, x, w1, b1, w2, b2, A, Bvec, Cmat, D, ln_w, ln_b, out):
    with ExitStack() as ctx:
        def sb(name, shape, dt=F32):
            return ctx.enter_context(nc.sbuf_tensor(name, shape, dt))

        def sem(name):
            return ctx.enter_context(nc.semaphore(name))

        xv = x.rearrange("b (h p) (r e) w -> b e h p r w", p=P, e=2)
        ov = out.rearrange("b (h p) (r e) w -> b e h p r w", p=P, e=2)

        id32 = sb("id32", [P, P])
        id16 = sb("id16", [P, P], F16)
        sel = sb("sel", [P, len(SEL_TAPS), (BROWS + 4) * COLS], F16)
        ones = sb("ones", [P, P])
        eps = sb("eps", [P, 1])
        W = sb("W", [P, 2, HALVES, STREAMS, TAPS], F16)
        bias = sb("bias", [P, 1])
        winv = sb("winv", [P, 1])
        yc = sb("yc", [P, HALVES, WIDTH])
        dcol = sb("dcol", [P, HALVES])
        lnw = sb("lnw", [P, HALVES])
        lnb = sb("lnb", [P, HALVES])
        raw = sb("raw", [P, 2, HALVES, PROWS, WIDTH])
        X = sb("X", [P, 2, HALVES, 2, ROWS, PCOLS], F16)
        V = sb("V", [P, 2, 2, HALVES, 2, VROWS, PCOLS], F16)
        HL = sb("HL", [P, 16, P], F16)
        AT = sb("AT", [P, 2, ROWS + 12, COLS], F16)
        raw_in = [sem("raw_in_even"), sem("raw_in_odd")]

        C = dict(id32=id32, id16=id16, sel=sel, ones=ones, eps=eps, W=W, bias=bias, winv=winv, yc=yc, dcol=dcol,
                 lnw=lnw, lnb=lnb, raw=raw, X=X, V=V, HL=HL, AT=AT, raw_in=raw_in,
                 xrows=lambda b, e, h: xv[b, e, h])
        prepare_weights(nc, sb, sem, C, w1, b1, w2, b2, A, Bvec, Cmat, D, ln_w, ln_b, x)

        T = sb("T", [P, 2, VROWS, WIDTH])
        Z = sb("Z", [P, TILE_ROWS, 2, COLS])
        E = sb("E", [P, 16, TAPS])
        st = sb("st", [P, 4, 16])
        XT = sb("XT", [P, 2, TILES, HALVES, P], F16)
        band = sb("band", [P, 2, TILES, BROWS, COLS], F16)
        tg = sb("tg", [P, HALVES, 16, WIDTH])
        o = sb("o", [P, 2, HALVES, 16, WIDTH])
        chs = sb("chs", [P, 2 * BANK])
        rs = sb("rs", [P, 2 * BANK])
        amx = sb("amx", [P, 2])
        aall = sb("aall", [P, 2])
        sc = sb("sc", [P, 2, 10])

        cv = ctx.enter_context(nc.psum_tensor("cv", [P, 2, BANK], F32))
        ms = ctx.enter_context(nc.psum_tensor("ms", [P, 2, BANK], F32))
        wk = ctx.enter_context(nc.psum_tensor("wk", [P, 4, BANK], F32))
        ms16 = ms[:].bitcast(F16)

        cv_zeroed = sem("cv_zeroed")
        amax_part, amax_all, scale_steps = sem("amax_part"), sem("amax_all"), sem("scale_steps")
        xhi, xlo = sem("x_high"), sem("x_low")
        tsum, vhi, vlo = sem("transform_sum"), sem("v_high"), sem("v_low")
        conv_done, z_evac = sem("conv_phase_done"), sem("logits_added")
        lt_ready, soft, exp_done = sem("logits_turned"), sem("softmax_steps"), sem("exp_done")
        hl_hi, ht_ready, at_copy = sem("att_high"), sem("att_turned"), sem("att_copied")
        sel_done, bhi, blo = sem("band_spread"), sem("band_high"), sem("band_low")
        y_done, t_made, gelu_done, o_made = sem("y_done"), sem("t_made"), sem("gelu_done"), sem("o_made")
        os_made, mean_done, d_made = sem("os_made"), sem("mean_done"), sem("centred")
        sq_made, ss_made, var_done = sem("squared"), sem("ss_made"), sem("var_done")
        ln_done, rstd, normed, affine = sem("ln_done"), sem("rstd"), sem("normed"), sem("affine_done")
        out_dma = sem("out_dma")
        xt_done, xt_high, xt_low = sem("x_turned"), sem("x_turned_high"), sem("x_turned_low")

        block = ctx.enter_context(nc.Block())

        @block.sync
        def _(sp):
            def unit(n, par, load=True, tail=True, first=False, b_load=None, b_out=None):
                if load:
                    if not first:
                        sp.wait_ge(tsum, 8 * n)
                        sp.wait_ge(xlo, 2 * n)
                        sp.wait_ge(xt_done, 8 * n)
                    for h in range(HALVES):
                        sp.dma_start(raw[:, 1 - par, h, PAD:PAD + ROWS, :],
                                     xv[b_load, 1 - par, h]).then_inc(raw_in[1 - par], 16)
                if tail:
                    for q in range(2):
                        for h in range(HALVES):
                            sp.wait_ge(affine, 4 * (n - 1) + 2 * q + h + 1)
                            sp.dma_start(ov[b_out, 1 - par, h, :, 16 * q:16 * q + 16, :], o[:, q, h]).then_inc(out_dma, 16)

            unit(0, 0, tail=False, first=True, b_load=0)
            for n in range(1, UNITS - 1):
                unit(n, n % 2, b_load=(n + 1) // 2, b_out=(n - 1) // 2)
            unit(7, 1, load=False, b_out=3)
            unit(8, 0, load=False, b_out=3)
            sp.wait_ge(out_dma, 64 * UNITS)

        @block.gpsimd
        def _(pool):
            def amax(n, par):
                pool.wait_ge(amax_part, n + 1)
                nc.gpsimd.partition_all_reduce(aall[:, par:par + 1], amx[:, par:par + 1], P, ABSMAX).then_inc(amax_all, 1)

            def unit(n, par, tail=True, prep=True):
                if tail:
                    m = n - 1
                    for q in range(2):
                        pool.wait_ge(o_made, 8 * m + 4 * q + 4)
                        if q:
                            pool.wait_ge(var_done, 2 * m + 1)
                        nc.gpsimd.tensor_tensor(chs[:, :], o[:, q, 0].rearrange("p r w -> p (r w)"),
                                                o[:, q, 1].rearrange("p r w -> p (r w)"), ALU.add).then_inc(os_made, 1)
                        pool.wait_ge(sq_made, 4 * m + 2 * q + 2)
                        pool.wait_ge(mean_done, 2 * m + q + 1)
                        nc.gpsimd.tensor_tensor(chs[:, :], tg[:, 0].rearrange("p r w -> p (r w)"),
                                                tg[:, 1].rearrange("p r w -> p (r w)"), ALU.add).then_inc(ss_made, 1)
                if prep:
                    amax(n + 1, 1 - par)
                if tail:
                    pool.wait_ge(var_done, 2 * n)

            amax(0, 0)
            unit(0, 0, tail=False)
            for n in range(1, UNITS - 1):
                unit(n, n % 2)
            unit(7, 1, prep=False)
            unit(8, 0, prep=False)

        @block.tensor
        def _(pe):
            def conv(n, first, last, warm=True):
                for step in range(first, last):
                    p = max(i for i in range(4) if PHASE_START[i] <= step)
                    j = step - PHASE_START[p]
                    if j == 0:
                        if warm or p >= 2:
                            pe.wait_ge(z_evac, 6 * n + (-2, 0, 1, 2)[p])
                        pe.wait_ge(vlo, 8 * n + 2 * p + 1)
                    if j == 14:
                        pe.wait_ge(vlo, 8 * n + 2 * p + 2)
                    if j < 28:
                        h, s = j // 14, j % 14
                        g, v, slot = s // K7, s % K7, p % 2
                        stream = 14 * TRANSFORM[p] + s
                        mov = lambda l, w: V[:, slot, l, h, w, 2 * g:2 * g + TILE_ROWS, v:v + COLS]
                    else:
                        if j == 28:
                            pe.wait_ge(xlo, 2 * n + 2)
                        h, v = (j - 28) // K7, (j - 28) % K7
                        stream = DIRECT + v
                        mov = lambda l, w: X[:, l, h, w, p:ROWS:2, v:v + COLS]
                    for k, (wl, xl) in enumerate(((0, 0), (0, 1), (1, 0))):
                        for w in range(2):
                            ins = pe.matmul(cv[LO * w:LO * w + TAPS, p % 2, :], W[:, wl, h, stream, :], mov(xl, w),
                                            start=(j == 0 and k == 0),
                                            stop=(j == PHASE_STEPS[p] - 1 and k == 2))
                    if j == PHASE_STEPS[p] - 1:
                        ins.then_inc(conv_done, 1)

            def turn_logits(m):
                pe.wait_ge(z_evac, 6 * m + 6)
                for t in range(8):
                    ins = pe.transpose(ms[:, t // 4, (t % 4) * P:(t % 4 + 1) * P],
                                       Z[:, 2 * t:2 * t + 2].rearrange("p a e c -> p (a e c)"), id32[:, :])
                ins.then_inc(lt_ready, 1)

            def turn_attention(m, g):
                pe.wait_ge(soft, 7 * m + 7)
                for t in range(4):
                    for w in range(2):
                        c = w * 4 * P + t * P
                        ins = pe.transpose(ms16[:, g, c:c + P], HL[:, (4 * g + t) * 2 + w, :], id16[:, :])
                ins.then_inc(ht_ready, 1)

            def spread(m, r):
                if r == 0:
                    pe.wait_ge(at_copy, 2 * m + 2)
                    pe.wait_ge(xt_low, 8 * m + 8)
                if r >= 4:
                    pe.wait_ge(blo, 10 * m + r - 3)
                for c in range(COLS):
                    s = c + 1 if c < PAD else c - COLS + 7 if c >= COLS - PAD else 0
                    f = (BROWS - 1 - r) * COLS + COLS - 1 - c
                    ins = pe.matmul(wk[:, r % 4, c * TILES:(c + 1) * TILES].rearrange("p (w j) -> p w j", w=2),
                                    sel[:, s, f:f + P],
                                    AT[:, :, r:r + 29:4, c], start=True, stop=True)
                ins.then_inc(sel_done, 1)

            def apply(m, y):
                q, h, w = y // 4, y // 2 % 2, y % 2
                if y == 0:
                    pe.wait_ge(blo, 10 * m + 10)
                if y >= 4:
                    pe.wait_ge(o_made, 8 * m + y - 3)
                begin = True
                for j in range(ROWS // 4):
                    r0, r1 = max(4 * j - PAD, 16 * q), min(4 * j + 4 + PAD, 16 * q + 16)
                    if r0 >= r1:
                        continue
                    for k, (xl, bl) in enumerate(((0, 0), (1, 0), (0, 1))):
                        ins = pe.matmul(wk[:, y % 4, (r0 - 16 * q) * COLS:(r1 - 16 * q) * COLS],
                                        XT[:, xl, 8 * w + j, h, :],
                                        band[:, bl, 8 * w + j, r0 - 4 * j + PAD:r1 - 4 * j + PAD, :]
                                        .rearrange("p r c -> p (r c)"),
                                        start=begin, stop=(k == 2 and r1 == 16 * q + 16 and 4 * j + 4 - PAD >= 16 * q + 13),
                                        skip_group_check=True)
                        begin = False
                ins.then_inc(y_done, 1)

            def mean(m, q):
                pe.wait_ge(os_made, 2 * m + q + 1)
                if q:
                    pe.wait_ge(ln_done, 2 * m + 1)
                for e in range(2):
                    ins = pe.matmul(ms[:, e, :], ones[:, :], chs[:, e * BANK:(e + 1) * BANK], start=True, stop=True)
                ins.then_inc(mean_done, 1)

            def variance(m, q):
                pe.wait_ge(ss_made, 2 * m + q + 1)
                pe.wait_ge(d_made, 4 * m + 2 * q + 2)
                for e in range(2):
                    ins = pe.matmul(ms[:, e, :], ones[:, :], chs[:, e * BANK:(e + 1) * BANK], start=True, stop=True)
                ins.then_inc(var_done, 1)

            def turn_x(n, par, g, warm=True):
                if g == 0 and warm:
                    pe.wait_ge(o_made, 8 * n)
                if g >= 4:
                    pe.wait_ge(xt_low, 8 * n + g - 3)
                for t in range(2):
                    for h in range(HALVES):
                        w, j = (2 * g + t) // 8, (2 * g + t) % 8
                        c = (t * HALVES + h) * P
                        rows = raw[:, par, h, PAD + 4 * j:PAD + 4 * j + 4, :].rearrange("p r w -> p (r w)")
                        ins = pe.transpose(wk[:, g % 4, c:c + P], rows[:, w:4 * WIDTH:2], id32[:, :])
                ins.then_inc(xt_done, 1)

            def unit(n, par):
                m = n - 1
                conv(n, 0, 3)
                turn_logits(m)
                conv(n, 3, 17)
                turn_attention(m, 0)
                turn_attention(m, 1)
                for r in range(BROWS):
                    conv(n, (17, 20)[r > 0] + 2 * max(r - 1, 0), 20 + 2 * r)
                    spread(m, r)
                for y in range(8):
                    conv(n, (38, 42)[y > 0] + 2 * max(y - 1, 0), 42 + 2 * y)
                    apply(m, y)
                conv(n, 56, 60)
                mean(m, 0)
                conv(n, 60, 68)
                variance(m, 0)
                conv(n, 68, 76)
                mean(m, 1)
                conv(n, 76, 84)
                variance(m, 1)
                for g in range(8):
                    conv(n, (84, 88)[g > 0] + 2 * max(g - 1, 0), 88 + 2 * g)
                    turn_x(n, par, g)
                conv(n, 102, 140)
                pe.wait_ge(ln_done, 2 * n)

            pe.wait_ge(cv_zeroed, 1)
            conv(0, 0, 42, warm=False)
            conv(0, 42, 84, warm=False)
            for g in range(8):
                turn_x(0, 0, g, warm=False)
            conv(0, 84, 140)
            with nc.tensor.Fori(0, UNITS // 2 - 1) as i:
                unit(2 * i + 1, 1)
                unit(2 * i + 2, 0)
            unit(UNITS - 1, 1)
            m = UNITS - 1
            turn_logits(m)
            turn_attention(m, 0)
            turn_attention(m, 1)
            for r in range(BROWS):
                spread(m, r)
            for y in range(8):
                apply(m, y)
            for q in range(2):
                mean(m, q)
                variance(m, q)

        @block.scalar
        def _(act):
            def v_high(n, par, p, cold=False):
                if not (cold and p < 2):
                    act.wait_ge(conv_done, 4 * n + p - 1)
                for h in range(HALVES):
                    act.wait_ge(tsum, 8 * n + 2 * p + h + 1)
                    nc.scalar.activation(V[:, p % 2, 0, h, :, :, PAD:PAD + COLS],
                                         T[:, h].rearrange("p r (c w) -> p w r c", w=2), ACT.Identity,
                                         scale=sc[:, par, 3:4]).then_inc(vhi, 1)

            def x_high(n, par):
                for h in range(HALVES):
                    nc.scalar.activation(X[:, 0, h, :, :, PAD:PAD + COLS],
                                         raw[:, par, h, PAD:PAD + ROWS, :].rearrange("p r (c w) -> p w r c", w=2),
                                         ACT.Identity, scale=sc[:, par, 3:4]).then_inc(xhi, 1)

            def turned_x(n, par):
                for g in range(8):
                    act.wait_ge(xt_done, 8 * n + g + 1)
                    nc.scalar.activation(XT[:, 0, 2 * g:2 * g + 2].rearrange("p t h c -> p (t h c)"), wk[:, g % 4, :],
                                         ACT.Identity, scale=sc[:, par, 3:4]).then_inc(xt_high, 1)

            def softmax(m):
                act.wait_ge(soft, 7 * m + 2)
                nc.scalar.activation(E[:, :, :], E[:, :, :], ACT.Exp).then_inc(exp_done, 1)
                act.wait_ge(soft, 7 * m + 6)
                nc.scalar.copy(HL[:, :, 0:TAPS], E[:, :, :]).then_inc(hl_hi, 1)

            def turned_attention(m):
                for g in range(2):
                    act.wait_ge(ht_ready, 2 * m + g + 1)
                    nc.scalar.copy(AT[:, :, PAD + 16 * g:PAD + 16 * g + 16, :].rearrange("p w r c -> p w (r c)"),
                                   ms16[:, g, :].rearrange("p (w f) -> p w f", w=2)).then_inc(at_copy, 1)

            def band_high(m):
                for r in range(BROWS):
                    act.wait_ge(sel_done, 10 * m + r + 1)
                    nc.scalar.copy(band[:, 0, :, r, :],
                                   wk[:, r % 4, :].rearrange("p (c t) -> p t c", t=TILES)).then_inc(bhi, 1)

            def gelus(m):
                for q in range(2):
                    for h in range(HALVES):
                        act.wait_ge(t_made, 8 * m + 4 * q + 2 * h + 2)
                        nc.scalar.activation(tg[:, h], tg[:, h], ACT.Gelu).then_inc(gelu_done, 1)

            def squares(m, q):
                act.wait_ge(o_made, 8 * m + 8)
                if q:
                    act.wait_ge(ss_made, 2 * m + 1)
                for h in range(HALVES):
                    act.wait_ge(d_made, 4 * m + 2 * q + h + 1)
                    nc.scalar.activation(tg[:, h], o[:, q, h], ACT.Square).then_inc(sq_made, 1)

            def finish(m, q):
                act.wait_ge(var_done, 2 * m + q + 1)
                nc.scalar.activation(rs[:, :], ms[:].rearrange("p a b -> p (a b)"), ACT.Ln,
                                     bias=eps[:, :]).then_inc(ln_done, 1)
                act.wait_ge(ln_done, 2 * m + q + 1)
                nc.scalar.activation(rs[:, :], rs[:, :], ACT.Exp, scale=-0.5).then_inc(rstd, 1)
                for h in range(HALVES):
                    act.wait_ge(normed, 4 * m + 2 * q + h + 1)
                    nc.scalar.activation(o[:, q, h], o[:, q, h], ACT.Identity, bias=lnb[:, h:h + 1],
                                         scale=lnw[:, h:h + 1]).then_inc(affine, 1)

            def prep(n, par, cold=False):
                act.wait_ge(scale_steps, 8 * n + 8)
                if not cold:
                    act.wait_ge(conv_done, 4 * n - 2)
                x_high(n, par)
                v_high(n, par, 0, cold)

            def unit(n, par, conv=True, nxt=True):
                m = n - 1
                softmax(m)
                turned_attention(m)
                if conv:
                    v_high(n, par, 1)
                band_high(m)
                gelus(m)
                if conv:
                    v_high(n, par, 2)
                for q in range(2):
                    squares(m, q)
                    finish(m, q)
                if conv:
                    v_high(n, par, 3)
                    turned_x(n, par)
                if nxt:
                    prep(n + 1, 1 - par)

            prep(0, 0, cold=True)
            v_high(0, 0, 1, cold=True)
            v_high(0, 0, 2)
            v_high(0, 0, 3)
            turned_x(0, 0)
            prep(1, 1)
            with nc.scalar.Fori(0, UNITS // 2 - 1) as i:
                unit(2 * i + 1, 1)
                unit(2 * i + 2, 0)
            unit(7, 1, nxt=False)
            unit(8, 0, conv=False, nxt=False)

        @block.vector
        def _(dve):
            def v_low(n, par, p, cold=False):
                r0, r1, op = ROW_PAIRS[TRANSFORM[p]]
                for h in range(HALVES):
                    if not (cold and p == 0):
                        dve.wait_ge(vlo, 8 * n + 2 * p + h - 1)
                    nc.vector.tensor_tensor(T[:, h], raw[:, par, h, r0:r0 + 2 * VROWS - 1:2, :],
                                            raw[:, par, h, r1:r1 + 2 * VROWS - 1:2, :], op).then_inc(tsum, 1)
                for h in range(HALVES):
                    dve.wait_ge(vhi, 8 * n + 2 * p + h + 1)
                    dve.wait_ge(tsum, 8 * n + 2 * p + h + 1)
                    nc.vector.scalar_tensor_tensor(
                        out=V[:, p % 2, 1, h, :, :, PAD:PAD + COLS], in0=T[:, h].rearrange("p r (c w) -> p w r c", w=2),
                        scalar=sc[:, par, 3:4], in1=V[:, p % 2, 0, h, :, :, PAD:PAD + COLS],
                        op0=ALU.mult, op1=ALU.subtract).then_inc(vlo, 1)

            def x_low(n, par):
                for h in range(HALVES):
                    dve.wait_ge(xhi, 2 * n + h + 1)
                    nc.vector.scalar_tensor_tensor(
                        out=X[:, 1, h, :, :, PAD:PAD + COLS],
                        in0=raw[:, par, h, PAD:PAD + ROWS, :].rearrange("p r (c w) -> p w r c", w=2),
                        scalar=sc[:, par, 3:4], in1=X[:, 0, h, :, :, PAD:PAD + COLS],
                        op0=ALU.mult, op1=ALU.subtract).then_inc(xlo, 1)

            def scales(n, par):
                dve.wait_ge(raw_in[par], 16 * (n - par) + 32)
                nc.vector.tensor_reduce(amx[:, par:par + 1], raw[:, par].rearrange("p h r w -> p (h r w)"), AX, ALU.max,
                                        apply_absolute_value=True).then_inc(amax_part, 1)
                dve.wait_ge(amax_all, n + 1)
                s = lambda c, k=1: sc[:, par, c:c + k]
                nc.vector.tensor_scalar(s(0), aall[:, par:par + 1], 1e-30, None, ALU.max).then_inc(scale_steps, 1)
                dve.wait_ge(scale_steps, 8 * n + 1)
                nc.vector.tensor_scalar(s(1).bitcast(U32), s(0).bitcast(U32), 0x7F800000, None,
                                        ALU.bitwise_and).then_inc(scale_steps, 1)
                dve.wait_ge(scale_steps, 8 * n + 2)
                nc.vector.reciprocal(s(2), s(1)).then_inc(scale_steps, 1)
                nc.vector.tensor_scalar(s(4), s(1), winv[:, :], 2.0 ** -13, ALU.mult, ALU.mult).then_inc(scale_steps, 1)
                nc.vector.tensor_scalar(s(6), s(1), 2.0 ** -13 / ATT_SCALE, None, ALU.mult).then_inc(scale_steps, 1)
                dve.wait_ge(scale_steps, 8 * n + 5)
                nc.vector.tensor_scalar(s(3), s(2), 2.0 ** 13, None, ALU.mult).then_inc(scale_steps, 1)
                nc.vector.tensor_scalar(s(5), s(4), -1.0, None, ALU.mult).then_inc(scale_steps, 1)
                nc.vector.tensor_scalar(s(7, 2), dcol[:, :], s(6), None, ALU.mult).then_inc(scale_steps, 1)
                dve.wait_ge(scale_steps, 8 * n + 8)

            def turned_x_low(n, par):
                for g in range(8):
                    dve.wait_ge(xt_high, 8 * n + g + 1)
                    low, high = (XT[:, l, 2 * g:2 * g + 2].rearrange("p t h c -> p (t h c)") for l in (1, 0))
                    nc.vector.scalar_tensor_tensor(out=low, in0=wk[:, g % 4, :], scalar=sc[:, par, 3:4], in1=high,
                                                   op0=ALU.mult, op1=ALU.subtract).then_inc(xt_low, 1)

            def add_logits(n, par, p, turned=True):
                dve.wait_ge(conv_done, 4 * n + p + 1)
                src = cv[:, p % 2, :].rearrange("p (r c) -> p r c", c=COLS)
                if p < 2:
                    if p == 0 and turned:
                        dve.wait_ge(lt_ready, n)
                    nc.vector.tensor_scalar(Z[:, :, p, :], src, sc[:, par, 4:5], bias[:, :], ALU.mult,
                                            ALU.add).then_inc(z_evac, 1)
                else:
                    dve.wait_ge(z_evac, 6 * n + (2, 4)[p - 2])
                    for e in range(2):
                        k = 5 if p == 3 and e == 1 else 4
                        nc.vector.scalar_tensor_tensor(out=Z[:, :, e, :], in0=src, scalar=sc[:, par, k:k + 1],
                                                       in1=Z[:, :, e, :], op0=ALU.mult, op1=ALU.add).then_inc(z_evac, 1)

            def softmax(m):
                dve.wait_ge(lt_ready, m + 1)
                logits = ms[:].rearrange("p b (i k) -> p (b i) k", k=LO)[:, :, 0:TAPS]
                wide = lambda c: st[:, c, :].unsqueeze(2).broadcast_to([P, 16, TAPS])
                nc.vector.tensor_reduce(st[:, 0, :], logits, AX, ALU.max).then_inc(soft, 1)
                dve.wait_ge(soft, 7 * m + 1)
                nc.vector.tensor_tensor(E[:, :, :], logits, wide(0), ALU.subtract).then_inc(soft, 1)
                dve.wait_ge(exp_done, m + 1)
                nc.vector.tensor_reduce(st[:, 1, :], E[:, :, :], AX, ALU.add).then_inc(soft, 1)
                dve.wait_ge(soft, 7 * m + 3)
                nc.vector.reciprocal(st[:, 2, :], st[:, 1, :]).then_inc(soft, 1)
                dve.wait_ge(soft, 7 * m + 4)
                nc.vector.tensor_scalar(st[:, 3, :], st[:, 2, :], ATT_SCALE, None, ALU.mult).then_inc(soft, 1)
                dve.wait_ge(soft, 7 * m + 5)
                nc.vector.tensor_tensor(E[:, :, :], E[:, :, :], wide(3), ALU.mult).then_inc(soft, 1)
                dve.wait_ge(hl_hi, m + 1)
                nc.vector.tensor_tensor(HL[:, :, LO:LO + TAPS], E[:, :, :], HL[:, :, 0:TAPS],
                                        ALU.subtract).then_inc(soft, 1)

            def band_low(m):
                for r in range(BROWS):
                    dve.wait_ge(bhi, 10 * m + r + 1)
                    nc.vector.tensor_tensor(band[:, 1, :, r, :], wk[:, r % 4, :].rearrange("p (c t) -> p t c", t=TILES),
                                            band[:, 0, :, r, :], ALU.subtract).then_inc(blo, 1)

            def outputs(m, par, q):
                for h in range(HALVES):
                    for w in range(2):
                        y = 4 * q + 2 * h + w
                        dve.wait_ge(y_done, 8 * m + y + 1)
                        nc.vector.scalar_tensor_tensor(
                            out=tg[:, h, :, w:WIDTH:2], in0=wk[:, y % 4, :].rearrange("p (r c) -> p r c", c=COLS),
                            scalar=sc[:, par, 7 + h:8 + h],
                            in1=yc[:, h, w:WIDTH:2].unsqueeze(1).broadcast_to([P, 16, COLS]),
                            op0=ALU.mult, op1=ALU.add).then_inc(t_made, 1)
                for h in range(HALVES):
                    dve.wait_ge(gelu_done, 4 * m + 2 * q + h + 1)
                    for w in range(2):
                        y = 4 * q + 2 * h + w
                        nc.vector.scalar_tensor_tensor(
                            out=o[:, q, h, :, w:WIDTH:2], in0=wk[:, y % 4, :].rearrange("p (r c) -> p r c", c=COLS),
                            scalar=sc[:, par, 6:7], in1=tg[:, h, :, w:WIDTH:2],
                            op0=ALU.mult, op1=ALU.add).then_inc(o_made, 1)
                dve.wait_ge(o_made, 8 * m + 4 * q + 4)

            def normalise(m, q):
                flat = lambda h: o[:, q, h].rearrange("p r w -> p (r w)")
                dve.wait_ge(mean_done, 2 * m + q + 1)
                dve.wait_ge(os_made, 2 * m + q + 1)
                for h in range(HALVES):
                    nc.vector.tensor_tensor(flat(h), flat(h), ms[:].rearrange("p a b -> p (a b)"),
                                            ALU.subtract).then_inc(d_made, 1)
                dve.wait_ge(rstd, 2 * m + q + 1)
                dve.wait_ge(sq_made, 4 * m + 2 * q + 2)
                for h in range(HALVES):
                    dve.wait_ge(d_made, 4 * m + 2 * q + h + 1)
                    nc.vector.tensor_tensor(flat(h), flat(h), rs[:, :], ALU.mult).then_inc(normed, 1)

            def prep(n, par, cold=False):
                x_low(n, par)
                v_low(n, par, 0, cold)

            def unit(n, par, conv=True, nxt=True):
                m = n - 1
                add_logits(m, 1 - par, 3)
                softmax(m)
                if conv:
                    v_low(n, par, 1)
                band_low(m)
                if conv:
                    add_logits(n, par, 0)
                outputs(m, 1 - par, 0)
                outputs(m, 1 - par, 1)
                if conv:
                    v_low(n, par, 2)
                normalise(m, 0)
                normalise(m, 1)
                if conv:
                    add_logits(n, par, 1)
                    v_low(n, par, 3)
                    turned_x_low(n, par)
                if nxt:
                    scales(n + 1, 1 - par)
                if conv:
                    add_logits(n, par, 2)
                if nxt:
                    prep(n + 1, 1 - par)
                dve.wait_ge(out_dma, 64 * n)
                dve.wait_ge(ss_made, 2 * n)

            nc.vector.memset(cv[:].rearrange("p a b -> p (a b)"), 0.0).then_inc(cv_zeroed, 1)
            scales(0, 0)
            prep(0, 0, cold=True)
            v_low(0, 0, 1)
            add_logits(0, 0, 0, turned=False)
            v_low(0, 0, 2)
            add_logits(0, 0, 1)
            v_low(0, 0, 3)
            turned_x_low(0, 0)
            scales(1, 1)
            add_logits(0, 0, 2)
            prep(1, 1)
            with nc.vector.Fori(0, UNITS // 2 - 1) as i:
                unit(2 * i + 1, 1)
                unit(2 * i + 2, 0)
            unit(7, 1, nxt=False)
            unit(8, 0, conv=False, nxt=False)


_INS = ["x", "L0_conv_w1", "L0_conv_b1", "L0_conv_w2", "L0_conv_b2", "L1_conv_A", "L1_conv_Bvec", "L1_conv_Cmat",
        "L1_conv_D", "L1_conv_ln_w", "L1_conv_ln_b"]
_OUT = (BATCH, CH, HEIGHT, WIDTH)


def kernel(**inputs):
    import numpy as _np
    import concourse.bacc as _bacc
    from concourse.bass_utils import run_bass_kernel_spmd as _run

    nc = _bacc.Bacc("TRN2", target_bir_lowering=False, num_devices=1)
    arrays, args = {}, []
    for name in _INS:
        a = _np.ascontiguousarray(inputs[name])
        arrays[f"in_{name}_dram"] = a
        args.append(nc.dram_tensor(f"in_{name}_dram", a.shape, mybir.dt.from_np(a.dtype), kind="ExternalInput").ap())
    args.append(nc.dram_tensor("out_0_dram", _OUT, F32, kind="ExternalOutput").ap())
    conv_seq_kernel(nc, *args)
    r = _run(nc, [arrays], core_ids=[0])
    return r.results[0]["out_0_dram"]
```

```python
from contextlib import ExitStack

import concourse.bass as bass
from concourse import mybir

F32 = mybir.dt.float32
F16 = mybir.dt.float16
U32 = mybir.dt.uint32
ALU = mybir.AluOpType
ACT = mybir.ActivationFunctionType
AX = mybir.AxisListType.X
ABSMAX = bass.bass_isa.ReduceOp.absmax

P = 128
BATCH, CH, HEIGHT, WIDTH = 4, 256, 64, 64
HALVES = CH // P
MID = 128
K7 = 7
TAPS = K7 * K7
ROWS, COLS = HEIGHT // 2, WIDTH // 2
PAD = 3
PROWS, PCOLS = ROWS + 2 * PAD, COLS + 2 * PAD
TILE_ROWS = ROWS // 2
VROWS = TILE_ROWS + 2
UNITS = BATCH * 2
STREAMS = 9 * K7
TILES = 2 * (ROWS // 4)
BROWS = 4 + 2 * PAD
BANK = 512
LO = 64
STATE = 32
LN_EPS = 1e-5
SEL_TAPS = ((0, 7), (3, 7), (2, 7), (1, 7), (0, 6), (0, 5), (0, 4))
SEL_AT = PAD * COLS + COLS - 1 - PAD
ATT_SCALE = 4096.0
COMPS = 9
GROUP = (0, 0, 1, 1, 2, 2, 3, 3, 4)
GROUP_END = (2, 4, 6, 8, 9)
COMP_STEPS = HALVES * K7
CONV_STEPS = COMPS * COMP_STEPS
RING = 3
SOURCE_ROW = (2, 0, 2, 1, 2, 0, 2, 0, 0)
T_STEP = (0, 1, None, 2, 3, 4, 5, 6, None)
X_SCALE = 2.0 ** 12
QUARTERS = 4
SCAN_STEPS = 6
MEAN_0, VARIANCE_0, MEAN_1, VARIANCE_1 = 58, 69, 72, 83


def conv_seq_kernel(nc, x, w1, b1, w2, b2, A, Bvec, Cmat, D, ln_w, ln_b, out):
    with ExitStack() as ctx:
        def sb(name, shape, dt=F32):
            return ctx.enter_context(nc.sbuf_tensor(name, shape, dt))

        def sem(name):
            return ctx.enter_context(nc.semaphore(name))

        xv = x.rearrange("b (h p) (r e) w -> b e h p r w", p=P, e=2)
        ov = out.rearrange("b (h p) (r e) w -> b e h p r w", p=P, e=2)

        id32 = sb("id32", [P, P])
        id16 = sb("id16", [P, P], F16)
        sel = sb("sel", [P, len(SEL_TAPS), (BROWS + 4) * COLS], F16)
        ones = sb("ones", [P, P])
        eps = sb("eps", [P, 1])
        W = sb("W", [P, 2, HALVES, STREAMS, TAPS], F16)
        bias = sb("bias", [P, 1])
        winv = sb("winv", [P, 1])
        yc = sb("yc", [P, HALVES, WIDTH])
        dcol = sb("dcol", [P, HALVES])
        lnw = sb("lnw", [P, HALVES])
        lnb = sb("lnb", [P, HALVES])
        raw = sb("raw", [P, 2, HALVES, PROWS, WIDTH])
        V = sb("V", [P, RING, 2, HALVES, 2, TILE_ROWS, PCOLS], F16)
        raw_in = [sem("raw_in_even"), sem("raw_in_odd")]
        T = sb("T", [P, HALVES, VROWS, WIDTH])
        A_rows = sb("A_rows", [P, HALVES, VROWS, WIDTH])
        amx = sb("amx", [P, 2, HALVES])
        aall = sb("aall", [P, 2, HALVES])
        sc = sb("sc", [P, 2, 10])

        with ExitStack() as early:
            def tmp(name, shape, dt=F32):
                return early.enter_context(nc.sbuf_tensor(name, shape, dt))

            def ptmp(name, shape):
                return early.enter_context(nc.psum_tensor(name, shape, F32))

            w1raw = tmp("w1raw", [P, HALVES, P * TAPS])
            wc = tmp("wc", [P, HALVES, K7, K7 * TAPS])
            ut = tmp("ut", [P, HALVES, 5, K7 * TAPS])
            w2raw = tmp("w2raw", [TAPS, MID])
            w2t = tmp("w2t", [MID, MID])
            b1col = tmp("b1col", [MID, 1])
            b2col = tmp("b2col", [P, 1])
            wmax = tmp("wmax", [P, HALVES * K7 + 1])
            wall = tmp("wall", [P, 1])
            wsc = tmp("wsc", [P, 8])
            powA = tmp("powA", [STATE, 2, 2, STATE])
            states = tmp("states", [STATE, WIDTH])
            cm = tmp("cm", [STATE, CH])
            pst = ptmp("pst", [P, 2, BANK])
            pcomp = ptmp("pcomp", [P, 3, 2 * BANK])

        HL = sb("HL", [P, 16, P], F16)
        AT = sb("AT", [P, 2, ROWS + 12, COLS], F16)
        Z = sb("Z", [P, TILE_ROWS, 2, COLS])
        E = sb("E", [P, 16, TAPS])
        st = sb("st", [P, 4, 16])
        XT = sb("XT", [P, 2, TILES, HALVES, P], F16)
        band = sb("band", [P, 2, TILES, BROWS, COLS], F16)
        tg = sb("tg", [P, HALVES, 16, WIDTH])
        o = sb("o", [P, 2, HALVES, 16, WIDTH])
        chs = sb("chs", [P, 2 * BANK])
        rs = sb("rs", [P, 2 * BANK])

        ms = ctx.enter_context(nc.psum_tensor("ms", [P, 2, BANK], F32))
        cv = ctx.enter_context(nc.psum_tensor("cv", [P, 2, BANK], F32))
        wk = ctx.enter_context(nc.psum_tensor("wk", [P, 4, BANK], F32))
        ms16 = ms[:].bitcast(F16)

        s_w1 = [sem("w1_in_0"), sem("w1_in_1")]
        s_w2, s_scan_in, s_d_in = sem("w2_in"), sem("scan_in"), sem("d_in")
        s_bias_in, s_norm_in = sem("biases_in"), sem("norm_in")
        s_ident, s_sel, s_const, s_border = sem("ident_set"), sem("select_set"), sem("constants_set"), sem("borders_set")
        s_b2z, s_w2z = sem("b2_cleared"), sem("w2t_cleared")
        s_w2t, s_w2s = sem("w2_turned"), sem("w2t_copied")
        s_comp, s_wcp, s_wmax, s_wall = sem("composite_ready"), sem("composite_copied"), sem("wmax_steps"), sem("wmax_all")
        s_wscale, s_u = sem("wscale_steps"), sem("row_transform_steps")
        w_high, w_low = sem("w_high"), sem("w_low")
        s_bsum, s_bias = sem("bias_summed"), sem("bias_steps")
        s_at, s_pow, s_powc = sem("a_turned"), sem("powers_ready"), sem("powers_copied")
        s_yc, s_ycc = sem("yc_ready"), sem("yc_copied")
        late_cleared = sem("late_cleared")

        cv_zeroed = sem("cv_zeroed")
        amax_part, amax_all, scale_steps = sem("amax_part"), sem("amax_all"), sem("scale_steps")
        a_made, e_again = sem("a_rows_made"), sem("e_rows_again")
        tsum, vhi, vlo = sem("transform_sum"), sem("v_high"), sem("v_low")
        conv_done, z_evac = sem("component_convolved"), sem("logits_added")
        lt_ready, soft, exp_done = sem("logits_turned"), sem("softmax_steps"), sem("exp_done")
        hl_hi, ht_ready, at_copy = sem("att_high"), sem("att_turned"), sem("att_copied")
        sel_done, bhi, blo = sem("band_spread"), sem("band_high"), sem("band_low")
        y_done, t_made, gelu_done, o_made = sem("y_done"), sem("t_made"), sem("gelu_done"), sem("o_made")
        os_made, mean_done, d_made = sem("os_made"), sem("mean_done"), sem("centred")
        sq_made, ss_made, var_done = sem("squared"), sem("ss_made"), sem("var_done")
        ln_done, rstd, normed, affine = sem("ln_done"), sem("rstd"), sem("normed"), sem("affine_done")
        out_dma = sem("out_dma")
        q_mean, q_centred, q_squared, q_var = sem("q_mean"), sem("q_centred"), sem("q_squared"), sem("q_var")
        q_ln, q_rstd, q_normed, q_done = sem("q_ln"), sem("q_rstd"), sem("q_normed"), [sem("q_done_0"), sem("q_done_1")]
        xt_done, xt_high, xt_low = sem("x_turned"), sem("x_turned_high"), sem("x_turned_low")

        WEIGHT_SOURCE = (("wc", 4, 3), ("wc", 0, 4), ("wc", 6, 3), ("wc", 3, 3), ("ut", 0, 4), ("ut", 1, 6),
                         ("ut", 2, 4), ("ut", 3, 7), ("ut", 4, 5))

        def weight_parts():
            for c, (which, i, scale) in enumerate(WEIGHT_SOURCE):
                for h in range(HALVES):
                    yield h, c, (wc if which == "wc" else ut)[:, h, i, :], scale

        def weight_set(low, h, c):
            return W[:, low, h, c * K7:(c + 1) * K7, :].rearrange("p v k -> p (v k)")

        def component(c, h):
            rows = T if T_STEP[c] is not None else A_rows
            return rows[:, h, SOURCE_ROW[c]:SOURCE_ROW[c] + TILE_ROWS, :].rearrange("p r (c w) -> p w r c", w=2)

        def component_ready(eng, n, c, h):
            if T_STEP[c] is None:
                eng.wait_ge(a_made, 2 * n + h + 1)
            else:
                eng.wait_ge(tsum, 14 * n + 2 * T_STEP[c] + h + 1)

        quarter = lambda t, i, h: t[:, i // 2, h, 8 * (i % 2):8 * (i % 2) + 8, :].rearrange("p r w -> p (r w)")
        square_of = lambda i, h: (tg, T)[i // 2][:, h, 8 * (i % 2):8 * (i % 2) + 8, :].rearrange("p r w -> p (r w)")
        column = lambda a: a.rearrange("(p o) -> p o", o=1)
        block = ctx.enter_context(nc.Block())

        @block.sync
        def _(sp):
            def unit(n, par, load=True, tail=True, first=False, b_load=None, b_out=None):
                if load:
                    if not first:
                        sp.wait_ge(tsum, 14 * n)
                        sp.wait_ge(xt_done, 8 * n)
                    for h in range(HALVES):
                        sp.dma_start(raw[:, 1 - par, h, PAD:PAD + ROWS, :],
                                     xv[b_load, 1 - par, h]).then_inc(raw_in[1 - par], 16)
                if tail:
                    for q in range(2):
                        for h in range(HALVES):
                            sp.wait_ge(affine, 4 * (n - 1) + 2 * q + h + 1)
                            sp.dma_start(ov[b_out, 1 - par, h, :, 16 * q:16 * q + 16, :], o[:, q, h]).then_inc(out_dma, 16)

            sp.dma_start(w2raw[:, :], w2.rearrange("k m a b -> k (m a b)")).then_inc(s_w2, 16)
            for h in range(HALVES):
                sp.dma_start(w1raw[:, h, :],
                             w1.rearrange("m (h c) a b -> h m (c a b)", h=HALVES)[h]).then_inc(s_w1[h], 16)
            for h in range(HALVES):
                sp.dma_start(raw[:, 0, h, PAD:PAD + ROWS, :], xv[0, 0, h]).then_inc(raw_in[0], 16)
            unit(0, 0, tail=False, first=True, b_load=0)
            for n in range(1, UNITS - 1):
                unit(n, n % 2, b_load=(n + 1) // 2, b_out=(n - 1) // 2)
            unit(7, 1, load=False, b_out=3)
            for i in range(QUARTERS):
                for h in range(HALVES):
                    sp.wait_ge(q_done[h], i + 1)
                    sp.dma_start(ov[BATCH - 1, 1, h, :, 8 * i:8 * i + 8, :],
                                 o[:, i // 2, h, 8 * (i % 2):8 * (i % 2) + 8, :]).then_inc(out_dma, 16)
            sp.wait_ge(out_dma, 64 * (UNITS - 1) + 16 * HALVES * QUARTERS)

        @block.gpsimd
        def _(pool):
            def amax(n, par):
                pool.wait_ge(amax_part, 2 * n + 2)
                nc.gpsimd.partition_all_reduce(aall[:, par, :], amx[:, par, :], P, ABSMAX).then_inc(amax_all, 1)

            def unit(n, par, tail=True, prep=True):
                if tail:
                    m = n - 1
                    for q in range(2):
                        pool.wait_ge(o_made, 8 * m + 4 * q + 4)
                        if q:
                            pool.wait_ge(var_done, 2 * m + 1)
                        nc.gpsimd.tensor_tensor(chs[:, :], o[:, q, 0].rearrange("p r w -> p (r w)"),
                                                o[:, q, 1].rearrange("p r w -> p (r w)"), ALU.add).then_inc(os_made, 1)
                        pool.wait_ge(sq_made, 4 * m + 2 * q + 2)
                        pool.wait_ge(mean_done, 2 * m + q + 1)
                        nc.gpsimd.tensor_tensor(chs[:, :], tg[:, 0].rearrange("p r w -> p (r w)"),
                                                tg[:, 1].rearrange("p r w -> p (r w)"), ALU.add).then_inc(ss_made, 1)
                if prep:
                    amax(n + 1, 1 - par)
                if tail:
                    pool.wait_ge(var_done, 2 * n)

            def constants():
                for n, t in enumerate((id32, id16)):
                    nc.gpsimd.memset(t[:, :], 0.0).then_inc(s_ident, 1)
                    pool.wait_ge(s_ident, 2 * n + 1)
                    nc.gpsimd.affine_select(out=t[:, :], in_=t[:, :], compare_op=ALU.not_equal, fill=1.0, base=0,
                                            pattern=[[-1, P]], channel_multiplier=1).then_inc(s_ident, 1)
                nc.gpsimd.memset(ones[:, :], 1.0 / CH).then_inc(s_const, 1)
                nc.gpsimd.memset(eps[:, :], LN_EPS).then_inc(s_const, 1)
                for slot in range(2):
                    for r in (0, PAD + ROWS):
                        nc.gpsimd.memset(raw[:, slot, :, r:r + PAD, :], 0.0).then_inc(s_border, 1)
                for c in (0, PAD + COLS):
                    nc.gpsimd.memset(V[:].rearrange("p s l h w r c -> p (s l h w r) c")[:, :, c:c + PAD],
                                     0.0).then_inc(s_border, 1)
                nc.gpsimd.memset(sel[:, :, :], 0.0).then_inc(s_sel, 1)
                for n, base in enumerate((0, -LO)):
                    pool.wait_ge(s_sel, 7 * n + 1)
                    for s, (v0, v1) in enumerate(SEL_TAPS):
                        v = sel[:, s, SEL_AT:SEL_AT + K7 * COLS].rearrange("p (u c) -> p u c", u=K7)[:, :, v0:v1]
                        nc.gpsimd.affine_select(out=v, in_=v, compare_op=ALU.not_equal, fill=1.0, base=base - v0,
                                                pattern=[[-K7, K7], [-1, v1 - v0]],
                                                channel_multiplier=1).then_inc(s_sel, 1)

            constants()
            pool.wait_ge(s_wmax, HALVES * K7 + 1)
            nc.gpsimd.partition_all_reduce(wall[:, :], wmax[:, HALVES * K7:], P, ABSMAX).then_inc(s_wall, 1)
            amax(0, 0)
            unit(0, 0, tail=False)
            for n in range(1, UNITS - 1):
                unit(n, n % 2)
            unit(7, 1, prep=False)

        @block.tensor
        def _(pe):
            def conv(n, par, first, last, warm=True):
                for step in range(first, last):
                    c, h, v = step // COMP_STEPS, step // K7 % HALVES, step % K7
                    g = GROUP[c]
                    group_first, group_last = c == 0 or GROUP[c - 1] != g, c + 1 == GROUP_END[g]
                    if step % COMP_STEPS == 0:
                        if group_first and (warm or g >= 2):
                            pe.wait_ge(z_evac, 8 * n + (-2, 0, 1, 2, 4)[g])
                        if not warm:
                            pe.wait_ge(w_low, 2 * c + 2)
                    if v == 0:
                        pe.wait_ge(vlo, 18 * n + 2 * c + h + 1)
                    for k, (wl, xl) in enumerate(((0, 0), (0, 1), (1, 0))):
                        for w in range(2):
                            ins = pe.matmul(cv[LO * w:LO * w + TAPS, (par + g) % 2, :], W[:, wl, h, c * K7 + v, :],
                                            V[:, c % RING, xl, h, w, :, v:v + COLS],
                                            start=(group_first and step % COMP_STEPS == 0 and k == 0),
                                            stop=(group_last and step % COMP_STEPS == COMP_STEPS - 1 and k == 2))
                    if step % COMP_STEPS == COMP_STEPS - 1:
                        ins.then_inc(conv_done, 1)

            def turn_logits(m):
                pe.wait_ge(z_evac, 8 * m + 8)
                for t in range(8):
                    ins = pe.transpose(ms[:, t // 4, (t % 4) * P:(t % 4 + 1) * P],
                                       Z[:, 2 * t:2 * t + 2].rearrange("p a e c -> p (a e c)"), id32[:, :])
                ins.then_inc(lt_ready, 1)

            def turn_attention(m, g):
                pe.wait_ge(soft, 7 * m + 7)
                for t in range(4):
                    for w in range(2):
                        c = w * 4 * P + t * P
                        ins = pe.transpose(ms16[:, g, c:c + P], HL[:, (4 * g + t) * 2 + w, :], id16[:, :])
                ins.then_inc(ht_ready, 1)

            def spread(m, r):
                if r == 0:
                    pe.wait_ge(at_copy, 2 * m + 2)
                    pe.wait_ge(xt_low, 8 * m + 8)
                if r >= 4:
                    pe.wait_ge(blo, 10 * m + r - 3)
                for c in range(COLS):
                    s = c + 1 if c < PAD else c - COLS + 7 if c >= COLS - PAD else 0
                    f = (BROWS - 1 - r) * COLS + COLS - 1 - c
                    ins = pe.matmul(wk[:, r % 4, c * TILES:(c + 1) * TILES].rearrange("p (w j) -> p w j", w=2),
                                    sel[:, s, f:f + P],
                                    AT[:, :, r:r + 29:4, c], start=True, stop=True)
                ins.then_inc(sel_done, 1)

            def apply(m, y):
                q, h, w = y // 4, y // 2 % 2, y % 2
                if y == 0:
                    pe.wait_ge(blo, 10 * m + 10)
                if y >= 4:
                    pe.wait_ge(o_made, 8 * m + y - 3)
                begin = True
                for j in range(ROWS // 4):
                    r0, r1 = max(4 * j - PAD, 16 * q), min(4 * j + 4 + PAD, 16 * q + 16)
                    if r0 >= r1:
                        continue
                    for k, (xl, bl) in enumerate(((0, 0), (1, 0), (0, 1))):
                        ins = pe.matmul(wk[:, y % 4, (r0 - 16 * q) * COLS:(r1 - 16 * q) * COLS],
                                        XT[:, xl, 8 * w + j, h, :],
                                        band[:, bl, 8 * w + j, r0 - 4 * j + PAD:r1 - 4 * j + PAD, :]
                                        .rearrange("p r c -> p (r c)"),
                                        start=begin, stop=(k == 2 and r1 == 16 * q + 16 and 4 * j + 4 - PAD >= 16 * q + 13),
                                        skip_group_check=True)
                        begin = False
                ins.then_inc(y_done, 1)

            def mean(m, q):
                pe.wait_ge(os_made, 2 * m + q + 1)
                if q:
                    pe.wait_ge(ln_done, 2 * m + 1)
                for e in range(2):
                    ins = pe.matmul(ms[:, e, :], ones[:, :], chs[:, e * BANK:(e + 1) * BANK], start=True, stop=True)
                ins.then_inc(mean_done, 1)

            def variance(m, q):
                pe.wait_ge(ss_made, 2 * m + q + 1)
                pe.wait_ge(d_made, 4 * m + 2 * q + 2)
                for e in range(2):
                    ins = pe.matmul(ms[:, e, :], ones[:, :], chs[:, e * BANK:(e + 1) * BANK], start=True, stop=True)
                ins.then_inc(var_done, 1)

            def turn_x(n, par, g, warm=True):
                if g == 0 and warm:
                    pe.wait_ge(o_made, 8 * n)
                if g >= 4:
                    pe.wait_ge(xt_low, 8 * n + g - 3)
                for t in range(2):
                    for h in range(HALVES):
                        w, j = (2 * g + t) // 8, (2 * g + t) % 8
                        c = (t * HALVES + h) * P
                        rows = raw[:, par, h, PAD + 4 * j:PAD + 4 * j + 4, :].rearrange("p r w -> p (r w)")
                        ins = pe.transpose(wk[:, g % 4, c:c + P], rows[:, w:4 * WIDTH:2], id32[:, :])
                ins.then_inc(xt_done, 1)

            def unit(n, par):
                m = n - 1
                conv(n, par, 0, 3)
                turn_logits(m)
                conv(n, par, 3, 17)
                turn_attention(m, 0)
                turn_attention(m, 1)
                for r in range(BROWS):
                    conv(n, par, (17, 20)[r > 0] + 2 * max(r - 1, 0), 20 + 2 * r)
                    spread(m, r)
                for y in range(8):
                    conv(n, par, (38, 42)[y > 0] + 2 * max(y - 1, 0), 42 + 2 * y)
                    apply(m, y)
                conv(n, par, 56, MEAN_0)
                mean(m, 0)
                conv(n, par, MEAN_0, VARIANCE_0)
                variance(m, 0)
                conv(n, par, VARIANCE_0, MEAN_1)
                mean(m, 1)
                conv(n, par, MEAN_1, VARIANCE_1)
                variance(m, 1)
                conv(n, par, VARIANCE_1, 84)
                for g in range(8):
                    conv(n, par, (84, 88)[g > 0] + 2 * max(g - 1, 0), 88 + 2 * g)
                    turn_x(n, par, g)
                conv(n, par, 102, CONV_STEPS)
                pe.wait_ge(ln_done, 2 * n)

            def scan_step(j):
                n = 1 << j
                pe.wait_ge(s_powc, 3 * j + 1)
                pe.matmul(pst[0:STATE, 0, 0:n], powA[:, j % 2, 1, :], states[:, 0:n], start=True, stop=True)
                pe.matmul(pst[0:STATE, 0, 64:96], powA[:, j % 2, 1, :], powA[:, j % 2, 0, :], start=True, stop=True)
                pe.matmul(pst[0:STATE, 0, 128:160], powA[:, j % 2, 0, :], powA[:, j % 2, 1, :],
                          start=True, stop=True).then_inc(s_pow, 1)

            def composite(g):
                h, u = g // K7, g % K7
                if u == 0:
                    pe.wait_ge(s_w1[h], 16)
                if g >= 3:
                    pe.wait_ge(s_wcp, g - 2)
                w1h = w1raw[:, h, :].rearrange("m (c t) -> m t c", t=TAPS)
                for v in range(K7):
                    last = pe.matmul(pcomp[:, g % 3, v * P:(v + 1) * P], w1h[:, u * K7 + v, :], w2t[:, :],
                                     start=True, stop=True)
                last.then_inc(s_comp, 1)

            pe.wait_ge(s_ident, 2)
            pe.wait_ge(s_w2, 16)
            pe.transpose(pst[:, 1, 0:TAPS], w2raw[:, :], id32[0:TAPS, 0:TAPS]).then_inc(s_w2t, 1)
            pe.wait_ge(s_w2s, 1)
            for g in range(K7):
                composite(g)
            pe.wait_ge(s_scan_in, 48)
            pe.transpose(pst[0:STATE, 0, 0:STATE], powA[:, 0, 0, :], id32[0:STATE, 0:STATE]).then_inc(s_at, 1)
            for g in range(K7, 2 * K7):
                composite(g)
                if g - K7 < SCAN_STEPS:
                    scan_step(g - K7)
            pe.wait_ge(s_powc, 3 * SCAN_STEPS + 1)
            for h in range(HALVES):
                last = pe.matmul(pst[:, 0, h * WIDTH:(h + 1) * WIDTH], cm[:, h * P:(h + 1) * P], states[:, :],
                                 start=True, stop=True)
            last.then_inc(s_yc, 1)
            pe.wait_ge(s_bias_in, 48)
            pe.matmul(pst[0:TAPS, 1, 0:1], w2t[:, 0:TAPS], b1col[:, :], start=True, stop=True)
            pe.matmul(pst[LO:LO + TAPS, 1, 0:1], w2t[:, 0:TAPS], b1col[:, :], start=True, stop=True).then_inc(s_bsum, 1)
            pe.wait_ge(s_border, 6)
            pe.wait_ge(cv_zeroed, 1)
            conv(0, 0, 0, 70, warm=False)
            pe.wait_ge(w_low, 2 * COMPS)
            for g in range(8):
                turn_x(0, 0, g, warm=False)
            conv(0, 0, 70, CONV_STEPS, warm=False)
            pe.wait_ge(s_sel, 15)
            pe.wait_ge(s_const, 2)
            with nc.tensor.Fori(0, UNITS // 2 - 1) as i:
                unit(2 * i + 1, 1)
                unit(2 * i + 2, 0)
            unit(UNITS - 1, 1)
            m = UNITS - 1
            turn_logits(m)
            turn_attention(m, 0)
            turn_attention(m, 1)
            for r in range(BROWS):
                spread(m, r)
            for y in range(8):
                apply(m, y)

            def last_mean(i):
                pe.wait_ge(o_made, 8 * m + 4 * (i // 2) + 4)
                if i >= 2:
                    pe.wait_ge(q_centred, 2 * (i - 2) + 2)
                for h in range(HALVES):
                    ins = pe.matmul(ms[:, i % 2, :], ones[:, :], quarter(o, i, h), start=(h == 0), stop=(h == 1))
                ins.then_inc(q_mean, 1)

            def last_variance(i):
                pe.wait_ge(q_squared, 2 * i + 2)
                if i >= 2:
                    pe.wait_ge(q_ln, i - 1)
                for h in range(HALVES):
                    ins = pe.matmul(cv[:, i % 2, :], ones[:, :], square_of(i, h), start=(h == 0), stop=(h == 1))
                ins.then_inc(q_var, 1)

            last_mean(0)
            last_mean(1)
            last_variance(0)
            last_mean(2)
            last_variance(1)
            last_mean(3)
            last_variance(2)
            last_variance(3)

        @block.scalar
        def _(act):
            def v_high(n, par, c, cold=False):
                if not (cold and c < RING):
                    act.wait_ge(conv_done, 9 * n + c - RING + 1)
                for h in range(HALVES):
                    component_ready(act, n, c, h)
                    nc.scalar.activation(V[:, c % RING, 0, h, :, :, PAD:PAD + COLS], component(c, h), ACT.Identity,
                                         scale=sc[:, par, 3:4]).then_inc(vhi, 1)

            def turned_x(n, par):
                for g in range(8):
                    act.wait_ge(xt_done, 8 * n + g + 1)
                    nc.scalar.activation(XT[:, 0, 2 * g:2 * g + 2].rearrange("p t h c -> p (t h c)"), wk[:, g % 4, :],
                                         ACT.Identity, scale=sc[:, par, 3:4]).then_inc(xt_high, 1)

            def softmax(m):
                act.wait_ge(soft, 7 * m + 2)
                nc.scalar.activation(E[:, :, :], E[:, :, :], ACT.Exp).then_inc(exp_done, 1)
                act.wait_ge(soft, 7 * m + 6)
                nc.scalar.copy(HL[:, :, 0:TAPS], E[:, :, :]).then_inc(hl_hi, 1)

            def turned_attention(m):
                for g in range(2):
                    act.wait_ge(ht_ready, 2 * m + g + 1)
                    nc.scalar.copy(AT[:, :, PAD + 16 * g:PAD + 16 * g + 16, :].rearrange("p w r c -> p w (r c)"),
                                   ms16[:, g, :].rearrange("p (w f) -> p w f", w=2)).then_inc(at_copy, 1)

            def band_high(m, rows=(0, BROWS)):
                for r in range(*rows):
                    act.wait_ge(sel_done, 10 * m + r + 1)
                    nc.scalar.copy(band[:, 0, :, r, :],
                                   wk[:, r % 4, :].rearrange("p (c t) -> p t c", t=TILES)).then_inc(bhi, 1)

            def gelus(m):
                for q in range(2):
                    for h in range(HALVES):
                        act.wait_ge(t_made, 8 * m + 4 * q + 2 * h + 2)
                        nc.scalar.activation(tg[:, h], tg[:, h], ACT.Gelu).then_inc(gelu_done, 1)

            def squares(m, q):
                act.wait_ge(o_made, 8 * m + 8)
                if q:
                    act.wait_ge(ss_made, 2 * m + 1)
                for h in range(HALVES):
                    act.wait_ge(d_made, 4 * m + 2 * q + h + 1)
                    nc.scalar.activation(tg[:, h], o[:, q, h], ACT.Square).then_inc(sq_made, 1)

            def finish(m, q):
                if q == 0:
                    act.preload_act_table_set("natural_log_exp_and_others")
                act.wait_ge(var_done, 2 * m + q + 1)
                nc.scalar.activation(rs[:, :], ms[:].rearrange("p a b -> p (a b)"), ACT.Ln,
                                     bias=eps[:, :]).then_inc(ln_done, 1)
                act.wait_ge(ln_done, 2 * m + q + 1)
                nc.scalar.activation(rs[:, :], rs[:, :], ACT.Exp, scale=-0.5).then_inc(rstd, 1)
                for h in range(HALVES):
                    act.wait_ge(normed, 4 * m + 2 * q + h + 1)
                    nc.scalar.activation(o[:, q, h], o[:, q, h], ACT.Identity, bias=lnb[:, h:h + 1],
                                         scale=lnw[:, h:h + 1]).then_inc(affine, 1)

            def prep(n, par):
                act.wait_ge(scale_steps, 9 * n + 9)
                v_high(n, par, 0)
                v_high(n, par, 1)

            def unit(n, par, nxt=True):
                m = n - 1
                softmax(m)
                v_high(n, par, 2)
                turned_attention(m)
                band_high(m, (0, 6))
                v_high(n, par, 3)
                band_high(m, (6, BROWS))
                v_high(n, par, 4)
                gelus(m)
                squares(m, 0)
                v_high(n, par, 5)
                finish(m, 0)
                squares(m, 1)
                v_high(n, par, 6)
                v_high(n, par, 7)
                finish(m, 1)
                v_high(n, par, 8)
                turned_x(n, par)
                if nxt:
                    prep(n + 1, 1 - par)

            def weights_high(first, last):
                for h, c, src, scale in list(weight_parts())[first:last]:
                    nc.scalar.activation(weight_set(0, h, c), src, ACT.Identity,
                                         scale=wsc[:, scale:scale + 1]).then_inc(w_high, 1)

            act.dma_start(powA[:, 0, 0, :], A).then_inc(s_scan_in, 16)
            act.dma_start(states[:, 0:1], column(Bvec)).then_inc(s_scan_in, 16)
            act.dma_start(cm[:, :], Cmat).then_inc(s_scan_in, 16)
            for h in range(HALVES):
                act.dma_start(dcol[:, h:h + 1], column(D[h * P:(h + 1) * P])).then_inc(s_d_in, 16)
            act.dma_start(b1col[:, :], column(b1)).then_inc(s_bias_in, 16)
            act.wait_ge(s_b2z, 1)
            for p0 in (0, LO):
                act.dma_start(b2col[p0:p0 + TAPS, :], column(b2)).then_inc(s_bias_in, 16)
            for dst, src in ((lnw, ln_w), (lnb, ln_b)):
                for h in range(HALVES):
                    act.dma_start(dst[:, h:h + 1], column(src[h * P:(h + 1) * P])).then_inc(s_norm_in, 16)
            for g in range(HALVES * K7):
                act.wait_ge(s_comp, g + 1)
                nc.scalar.copy(wc[:, g // K7, g % K7, :].rearrange("p (v k) -> p v k", v=K7),
                               pcomp[:, g % 3, 0:K7 * P].rearrange("p (v k) -> p v k", v=K7)[:, :, 0:TAPS]
                               ).then_inc(s_wcp, 1)
            act.wait_ge(s_wscale, 9)
            weights_high(0, 2)
            act.wait_ge(scale_steps, 9)
            v_high(0, 0, 0, cold=True)
            weights_high(2, 4)
            v_high(0, 0, 1, cold=True)
            weights_high(4, 6)
            v_high(0, 0, 2, cold=True)
            weights_high(6, 8)
            act.wait_ge(s_const, 2)
            act.wait_ge(s_norm_in, 64)
            act.wait_ge(s_u, 20)
            weights_high(8, 18)
            v_high(0, 0, 3)
            v_high(0, 0, 4)
            v_high(0, 0, 5)
            v_high(0, 0, 6)
            act.wait_ge(w_low, 2 * COMPS)
            turned_x(0, 0)
            v_high(0, 0, 7)
            v_high(0, 0, 8)
            prep(1, 1)
            act.wait_ge(late_cleared, 2)
            act.preload_act_table_set("natural_log_exp_and_others")
            with nc.scalar.Fori(0, UNITS // 2 - 1) as i:
                unit(2 * i + 1, 1)
                unit(2 * i + 2, 0)
            unit(7, 1, nxt=False)
            m = UNITS - 1
            softmax(m)
            turned_attention(m)
            band_high(m)
            gelus(m)
            act.preload_act_table_set("natural_log_exp_and_others")

            def last_squares(i):
                act.wait_ge(o_made, 8 * m + 8)
                for h in range(HALVES):
                    act.wait_ge(q_centred, 2 * i + h + 1)
                    nc.scalar.activation(square_of(i, h), quarter(o, i, h), ACT.Square).then_inc(q_squared, 1)

            def last_rstd(i):
                act.wait_ge(q_var, i + 1)
                if i >= 2:
                    act.wait_ge(q_normed, 2 * (i - 2) + 2)
                r = rs[:, (i % 2) * BANK:(i % 2 + 1) * BANK]
                nc.scalar.activation(r, cv[:, i % 2, :], ACT.Ln, bias=eps[:, :]).then_inc(q_ln, 1)
                act.wait_ge(q_ln, i + 1)
                nc.scalar.activation(r, r, ACT.Exp, scale=-0.5).then_inc(q_rstd, 1)

            def last_affine(i):
                act.wait_ge(q_normed, 2 * i + 1)
                nc.scalar.activation(quarter(o, i, 0), quarter(o, i, 0), ACT.Identity, bias=lnb[:, 0:1],
                                     scale=lnw[:, 0:1]).then_inc(q_done[0], 1)

            last_squares(0)
            last_squares(1)
            for i in range(QUARTERS):
                last_rstd(i)
                if i + 2 < QUARTERS:
                    last_squares(i + 2)
                last_affine(i)

        @block.vector
        def _(dve):
            def paired(dst, par, h, r, rows, pair, op):
                return nc.vector.tensor_tensor(dst[:, h, r:r + rows],
                                               *(raw[:, par, h, 2 * r + d:2 * r + d + 2 * rows - 1:2, :] for d in pair), op)

            def a_rows(n, par, cold=False):
                for h in range(HALVES):
                    if not cold:
                        dve.wait_ge(vlo, 18 * n + h - 1)
                    paired(A_rows, par, h, 0, VROWS, (3, 1), ALU.subtract).then_inc(a_made, 1)

            def t_rows(n, par, c, cold=False):
                pair, op = {0: ((0, 2), ALU.subtract), 4: ((1, 2), ALU.add), 6: ((2, 1), ALU.subtract)}[c]
                for h in range(HALVES):
                    if not cold:
                        dve.wait_ge(vlo, 18 * n + {0: -4, 4: 6, 6: 10}[c] + h + 1)
                    paired(T, par, h, 0, VROWS, pair, op).then_inc(tsum, 1)

            def e_rows_again(n, par):
                for h in range(HALVES):
                    dve.wait_ge(vlo, 18 * n + 2 + h + 1)
                    paired(T, par, h, 1, TILE_ROWS, (0, 2), ALU.subtract).then_inc(e_again, 1)

            def combine(n, c):
                for h in range(HALVES):
                    if c == 3:
                        dve.wait_ge(e_again, 2 * n + h + 1)
                    else:
                        dve.wait_ge(vlo, 18 * n + 2 * (c - 1) + h + 1)
                        dve.wait_ge(tsum, 14 * n + 2 * T_STEP[c - 1] + h + 1)
                    dve.wait_ge(a_made, 2 * n + h + 1)
                    r = SOURCE_ROW[c]
                    t, a = T[:, h, r:r + TILE_ROWS, :], A_rows[:, h, 0:TILE_ROWS, :]
                    if c == 1:
                        ins = nc.vector.scalar_tensor_tensor(out=t, in0=t, scalar=2.0, in1=a, op0=ALU.mult, op1=ALU.add)
                    elif c == 3:
                        ins = nc.vector.scalar_tensor_tensor(out=t, in0=a, scalar=-2.0, in1=t, op0=ALU.mult,
                                                             op1=ALU.subtract)
                    elif c == 5:
                        ins = nc.vector.tensor_tensor(t, a, t, ALU.subtract)
                    else:
                        ins = nc.vector.scalar_tensor_tensor(out=t, in0=t, scalar=-3.0, in1=a, op0=ALU.mult, op1=ALU.add)
                    ins.then_inc(tsum, 1)

            def v_low(n, par, c):
                for h in range(HALVES):
                    dve.wait_ge(vhi, 18 * n + 2 * c + h + 1)
                    component_ready(dve, n, c, h)
                    nc.vector.scalar_tensor_tensor(
                        out=V[:, c % RING, 1, h, :, :, PAD:PAD + COLS], in0=component(c, h),
                        scalar=sc[:, par, 3:4], in1=V[:, c % RING, 0, h, :, :, PAD:PAD + COLS],
                        op0=ALU.mult, op1=ALU.subtract).then_inc(vlo, 1)

            def scales(n, par, part=0):
                if part != 2:
                    dve.wait_ge(raw_in[par], 16 * (n - par) + 32)
                    for h in range(HALVES):
                        nc.vector.tensor_reduce(amx[:, par, h:h + 1],
                                                raw[:, par, h, PAD:PAD + ROWS, :].rearrange("p r w -> p (r w)"), AX,
                                                ALU.max, apply_absolute_value=True).then_inc(amax_part, 1)
                if part == 1:
                    return
                dve.wait_ge(amax_all, n + 1)
                s = lambda c, k=1: sc[:, par, c:c + k]
                nc.vector.tensor_scalar(s(0), aall[:, par, 0:1], aall[:, par, 1:2], 1e-30, ALU.max,
                                        ALU.max).then_inc(scale_steps, 1)
                dve.wait_ge(scale_steps, 9 * n + 1)
                nc.vector.tensor_scalar(s(1).bitcast(U32), s(0).bitcast(U32), 0x7F800000, None,
                                        ALU.bitwise_and).then_inc(scale_steps, 1)
                dve.wait_ge(scale_steps, 9 * n + 2)
                nc.vector.reciprocal(s(2), s(1)).then_inc(scale_steps, 1)
                nc.vector.tensor_scalar(s(4), s(1), winv[:, :], 1 / X_SCALE, ALU.mult, ALU.mult).then_inc(scale_steps, 1)
                nc.vector.tensor_scalar(s(6), s(1), 1 / (X_SCALE * ATT_SCALE), None, ALU.mult).then_inc(scale_steps, 1)
                dve.wait_ge(scale_steps, 9 * n + 5)
                nc.vector.tensor_scalar(s(3), s(2), X_SCALE, None, ALU.mult).then_inc(scale_steps, 1)
                nc.vector.tensor_scalar(s(5), s(4), -1.0, None, ALU.mult).then_inc(scale_steps, 1)
                nc.vector.tensor_scalar(s(9), s(4), 2.0, None, ALU.mult).then_inc(scale_steps, 1)
                nc.vector.tensor_scalar(s(7, 2), dcol[:, :], s(6), None, ALU.mult).then_inc(scale_steps, 1)
                dve.wait_ge(scale_steps, 9 * n + 9)

            def turned_x_low(n, par, groups=(0, 8)):
                for g in range(*groups):
                    dve.wait_ge(xt_high, 8 * n + g + 1)
                    low, high = (XT[:, l, 2 * g:2 * g + 2].rearrange("p t h c -> p (t h c)") for l in (1, 0))
                    nc.vector.scalar_tensor_tensor(out=low, in0=wk[:, g % 4, :], scalar=sc[:, par, 3:4], in1=high,
                                                   op0=ALU.mult, op1=ALU.subtract).then_inc(xt_low, 1)

            def add_logits(n, par, g, turned=True):
                dve.wait_ge(conv_done, 9 * n + GROUP_END[g])
                src = cv[:, (par + g) % 2, :].rearrange("p (r c) -> p r c", c=COLS)
                if g < 2:
                    if g == 0 and turned:
                        dve.wait_ge(lt_ready, n)
                    nc.vector.tensor_scalar(Z[:, :, g, :], src, sc[:, par, 4:5], bias[:, :], ALU.mult,
                                            ALU.add).then_inc(z_evac, 1)
                else:
                    dve.wait_ge(z_evac, 8 * n + 2 * g - 2)
                    for e, k in enumerate(((4, 4), (4, 5), (4, 9))[g - 2]):
                        nc.vector.scalar_tensor_tensor(out=Z[:, :, e, :], in0=src, scalar=sc[:, par, k:k + 1],
                                                       in1=Z[:, :, e, :], op0=ALU.mult, op1=ALU.add).then_inc(z_evac, 1)

            def softmax(m):
                dve.wait_ge(lt_ready, m + 1)
                logits = ms[:].rearrange("p b (i k) -> p (b i) k", k=LO)[:, :, 0:TAPS]
                wide = lambda c: st[:, c, :].unsqueeze(2).broadcast_to([P, 16, TAPS])
                nc.vector.tensor_reduce(st[:, 0, :], logits, AX, ALU.max).then_inc(soft, 1)
                dve.wait_ge(soft, 7 * m + 1)
                nc.vector.tensor_tensor(E[:, :, :], logits, wide(0), ALU.subtract).then_inc(soft, 1)
                dve.wait_ge(exp_done, m + 1)
                nc.vector.tensor_reduce(st[:, 1, :], E[:, :, :], AX, ALU.add).then_inc(soft, 1)
                dve.wait_ge(soft, 7 * m + 3)
                nc.vector.reciprocal(st[:, 2, :], st[:, 1, :]).then_inc(soft, 1)
                dve.wait_ge(soft, 7 * m + 4)
                nc.vector.tensor_scalar(st[:, 3, :], st[:, 2, :], ATT_SCALE, None, ALU.mult).then_inc(soft, 1)
                dve.wait_ge(soft, 7 * m + 5)
                nc.vector.tensor_tensor(E[:, :, :], E[:, :, :], wide(3), ALU.mult).then_inc(soft, 1)
                dve.wait_ge(hl_hi, m + 1)
                nc.vector.tensor_tensor(HL[:, :, LO:LO + TAPS], E[:, :, :], HL[:, :, 0:TAPS],
                                        ALU.subtract).then_inc(soft, 1)

            def band_low(m, rows=(0, BROWS)):
                for r in range(*rows):
                    dve.wait_ge(bhi, 10 * m + r + 1)
                    nc.vector.tensor_tensor(band[:, 1, :, r, :], wk[:, r % 4, :].rearrange("p (c t) -> p t c", t=TILES),
                                            band[:, 0, :, r, :], ALU.subtract).then_inc(blo, 1)

            def outputs(m, par, q):
                for h in range(HALVES):
                    for w in range(2):
                        y = 4 * q + 2 * h + w
                        dve.wait_ge(y_done, 8 * m + y + 1)
                        nc.vector.scalar_tensor_tensor(
                            out=tg[:, h, :, w:WIDTH:2], in0=wk[:, y % 4, :].rearrange("p (r c) -> p r c", c=COLS),
                            scalar=sc[:, par, 7 + h:8 + h],
                            in1=yc[:, h, w:WIDTH:2].unsqueeze(1).broadcast_to([P, 16, COLS]),
                            op0=ALU.mult, op1=ALU.add).then_inc(t_made, 1)
                for h in range(HALVES):
                    dve.wait_ge(gelu_done, 4 * m + 2 * q + h + 1)
                    for w in range(2):
                        y = 4 * q + 2 * h + w
                        nc.vector.scalar_tensor_tensor(
                            out=o[:, q, h, :, w:WIDTH:2], in0=wk[:, y % 4, :].rearrange("p (r c) -> p r c", c=COLS),
                            scalar=sc[:, par, 6:7], in1=tg[:, h, :, w:WIDTH:2],
                            op0=ALU.mult, op1=ALU.add).then_inc(o_made, 1)
                dve.wait_ge(o_made, 8 * m + 4 * q + 4)

            flat = lambda a: a.rearrange("p r w -> p (r w)")

            def centre(m, q):
                dve.wait_ge(mean_done, 2 * m + q + 1)
                dve.wait_ge(os_made, 2 * m + q + 1)
                for h in range(HALVES):
                    nc.vector.tensor_tensor(flat(o[:, q, h]), flat(o[:, q, h]), ms[:].rearrange("p a b -> p (a b)"),
                                            ALU.subtract).then_inc(d_made, 1)

            def normalise(m, q):
                dve.wait_ge(rstd, 2 * m + q + 1)
                dve.wait_ge(sq_made, 4 * m + 2 * q + 2)
                for h in range(HALVES):
                    dve.wait_ge(d_made, 4 * m + 2 * q + h + 1)
                    nc.vector.tensor_tensor(flat(o[:, q, h]), flat(o[:, q, h]), rs[:, :], ALU.mult).then_inc(normed, 1)

            def unit(n, par, nxt=True):
                m = n - 1
                add_logits(m, 1 - par, 4)
                softmax(m)
                v_low(n, par, 2)
                if nxt:
                    scales(n + 1, 1 - par, part=1)
                band_low(m, (0, 2))
                e_rows_again(n, par)
                band_low(m, (2, 4))
                combine(n, 3)
                band_low(m, (4, 6))
                v_low(n, par, 3)
                band_low(m, (6, BROWS))
                t_rows(n, par, 4)
                add_logits(n, par, 0)
                v_low(n, par, 4)
                outputs(m, 1 - par, 0)
                outputs(m, 1 - par, 1)
                add_logits(n, par, 1)
                centre(m, 0)
                combine(n, 5)
                v_low(n, par, 5)
                normalise(m, 0)
                centre(m, 1)
                t_rows(n, par, 6)
                v_low(n, par, 6)
                combine(n, 7)
                v_low(n, par, 7)
                normalise(m, 1)
                add_logits(n, par, 2)
                v_low(n, par, 8)
                turned_x_low(n, par, (0, 2))
                if nxt:
                    t_rows(n + 1, 1 - par, 0)
                turned_x_low(n, par, (2, 4))
                if nxt:
                    a_rows(n + 1, 1 - par)
                turned_x_low(n, par, (4, 6))
                if nxt:
                    scales(n + 1, 1 - par, part=2)
                turned_x_low(n, par, (6, 8))
                if nxt:
                    v_low(n + 1, 1 - par, 0)
                    combine(n + 1, 1)
                add_logits(n, par, 3)
                if nxt:
                    v_low(n + 1, 1 - par, 1)
                dve.wait_ge(out_dma, 64 * n)
                dve.wait_ge(ss_made, 2 * n)

            def scan_copies(j):
                n = 1 << j
                dve.wait_ge(s_pow, j + 1)
                nc.vector.tensor_scalar(states[:, n:2 * n], pst[0:STATE, 0, 0:n], states[:, n - 1:n], None,
                                        ALU.add).then_inc(s_powc, 1)
                nc.vector.tensor_copy(powA[:, (j + 1) % 2, 0, :], pst[0:STATE, 0, 64:96]).then_inc(s_powc, 1)
                nc.vector.tensor_copy(powA[:, (j + 1) % 2, 1, :], pst[0:STATE, 0, 128:160]).then_inc(s_powc, 1)
                dve.wait_ge(s_powc, 3 * j + 4)

            def composite_max(g):
                h, u = g // K7, g % K7
                dve.wait_ge(s_wcp, g + 1)
                nc.vector.tensor_reduce(wmax[:, g:g + 1], wc[:, h, u, :], AX, ALU.max,
                                        apply_absolute_value=True).then_inc(s_wmax, 1)

            def row_sums(h):
                g = lambda u: wc[:, h, u, :]
                u = lambda i: ut[:, h, i, :]
                add, sub = ALU.add, ALU.subtract
                done = 10 * h
                nc.vector.tensor_tensor(u(2), g(4), g(6), add).then_inc(s_u, 1)
                nc.vector.tensor_tensor(u(3), g(0), g(2), add).then_inc(s_u, 1)
                nc.vector.tensor_tensor(u(1), g(1), g(3), add).then_inc(s_u, 1)
                nc.vector.scalar_tensor_tensor(out=u(4), in0=g(3), scalar=2.0, in1=g(2), op0=ALU.mult,
                                               op1=add).then_inc(s_u, 1)
                dve.wait_ge(s_u, done + 4)
                nc.vector.tensor_tensor(u(0), u(2), g(5), add).then_inc(s_u, 1)
                nc.vector.tensor_tensor(u(2), u(2), g(5), sub).then_inc(s_u, 1)
                nc.vector.scalar_tensor_tensor(out=u(4), in0=u(4), scalar=2.0, in1=g(1), op0=ALU.mult,
                                               op1=add).then_inc(s_u, 1)
                nc.vector.tensor_tensor(u(1), u(3), u(1), add).then_inc(s_u, 1)
                dve.wait_ge(s_u, done + 8)
                nc.vector.scalar_tensor_tensor(out=u(3), in0=u(3), scalar=2.0, in1=u(1), op0=ALU.mult,
                                               op1=sub).then_inc(s_u, 1)
                nc.vector.scalar_tensor_tensor(out=u(4), in0=u(4), scalar=2.0, in1=g(0), op0=ALU.mult,
                                               op1=add).then_inc(s_u, 1)

            def weight_scales():
                dve.wait_ge(s_wall, 1)
                nc.vector.tensor_scalar(wsc[:, 0:1], wall[:, :], 1e-30, None, ALU.max).then_inc(s_wscale, 1)
                dve.wait_ge(s_wscale, 1)
                nc.vector.tensor_scalar(wsc[:, 1:2].bitcast(U32), wsc[:, 0:1].bitcast(U32), 0x7F800000, None,
                                        ALU.bitwise_and).then_inc(s_wscale, 1)
                dve.wait_ge(s_wscale, 2)
                nc.vector.reciprocal(wsc[:, 2:3], wsc[:, 1:2]).then_inc(s_wscale, 1)
                nc.vector.tensor_scalar(winv[:, :], wsc[:, 1:2], 2.0 ** -13, None, ALU.mult).then_inc(s_wscale, 1)
                dve.wait_ge(s_wscale, 4)
                nc.vector.tensor_scalar(wsc[:, 3:4], wsc[:, 2:3], 2.0 ** 13, None, ALU.mult).then_inc(s_wscale, 1)
                for column, factor in ((4, 0.5), (5, 1 / 6), (6, -0.5), (7, -1 / 6)):
                    nc.vector.tensor_scalar(wsc[:, column:column + 1], wsc[:, 2:3], 2.0 ** 13 * factor, None,
                                            ALU.mult).then_inc(s_wscale, 1)
                dve.wait_ge(s_wscale, 9)

            def weights_low(first, last):
                for n, (h, c, src, scale) in list(enumerate(weight_parts()))[first:last]:
                    dve.wait_ge(w_high, n + 1)
                    nc.vector.scalar_tensor_tensor(out=weight_set(1, h, c), in0=src, scalar=wsc[:, scale:scale + 1],
                                                   in1=weight_set(0, h, c), op0=ALU.mult,
                                                   op1=ALU.subtract).then_inc(w_low, 1)

            nc.vector.memset(b2col[:, :], 0.0).then_inc(s_b2z, 1)
            nc.vector.memset(w2t[:, :], 0.0).then_inc(s_w2z, 1)
            dve.wait_ge(s_w2z, 1)
            dve.wait_ge(s_w2t, 1)
            nc.vector.tensor_copy(w2t[:, 0:TAPS], pst[:, 1, 0:TAPS]).then_inc(s_w2s, 1)
            for g in range(K7):
                composite_max(g)
            dve.wait_ge(s_at, 1)
            nc.vector.tensor_copy(powA[:, 0, 1, :], pst[0:STATE, 0, 0:STATE]).then_inc(s_powc, 1)
            for g in range(K7, 2 * K7):
                composite_max(g)
                if g - K7 < SCAN_STEPS:
                    scan_copies(g - K7)
                if g == 2 * K7 - 3:
                    scales(0, 0, part=1)
                if g == 2 * K7 - 2:
                    nc.vector.memset(cv[:].rearrange("p a b -> p (a b)"), 0.0).then_inc(cv_zeroed, 1)
            dve.wait_ge(s_wmax, HALVES * K7)
            nc.vector.tensor_reduce(wmax[:, HALVES * K7:], wmax[:, 0:HALVES * K7], AX, ALU.max).then_inc(s_wmax, 1)
            dve.wait_ge(s_border, 6)
            t_rows(0, 0, 0, cold=True)
            weight_scales()
            dve.wait_ge(s_d_in, 32)
            scales(0, 0, part=2)
            weights_low(0, 2)
            v_low(0, 0, 0)
            a_rows(0, 0, cold=True)
            combine(0, 1)
            weights_low(2, 4)
            v_low(0, 0, 1)
            weights_low(4, 6)
            v_low(0, 0, 2)
            weights_low(6, 8)
            row_sums(0)
            row_sums(1)
            e_rows_again(0, 0)
            combine(0, 3)
            dve.wait_ge(s_yc, 1)
            nc.vector.tensor_copy(yc[:, :, :], pst[:, 0, 0:HALVES * WIDTH].rearrange(
                "p (h w) -> p h w", h=HALVES)).then_inc(s_ycc, 1)
            dve.wait_ge(s_bsum, 1)
            nc.vector.tensor_copy(bias[:, :], b2col[:, :]).then_inc(s_bias, 1)
            dve.wait_ge(s_bias, 1)
            for p0 in (0, LO):
                nc.vector.tensor_tensor(bias[p0:p0 + TAPS, :], b2col[p0:p0 + TAPS, :], pst[p0:p0 + TAPS, 1, 0:1],
                                        ALU.add).then_inc(s_bias, 1)
            weights_low(8, 18)
            v_low(0, 0, 3)
            dve.wait_ge(w_low, 18)
            nc.vector.memset(HL[:].rearrange("p i k -> p (i k)").bitcast(U32), 0).then_inc(late_cleared, 1)
            nc.vector.memset(AT[:].rearrange("p w r c -> p (w r c)").bitcast(U32), 0).then_inc(late_cleared, 1)
            dve.wait_ge(late_cleared, 2)
            dve.wait_ge(s_bias, 3)
            t_rows(0, 0, 4)
            v_low(0, 0, 4)
            add_logits(0, 0, 0, turned=False)
            combine(0, 5)
            v_low(0, 0, 5)
            add_logits(0, 0, 1)
            t_rows(0, 0, 6)
            v_low(0, 0, 6)
            turned_x_low(0, 0)
            combine(0, 7)
            v_low(0, 0, 7)
            add_logits(0, 0, 2)
            v_low(0, 0, 8)
            scales(1, 1)
            t_rows(1, 1, 0)
            a_rows(1, 1)
            v_low(1, 1, 0)
            combine(1, 1)
            add_logits(0, 0, 3)
            v_low(1, 1, 1)
            with nc.vector.Fori(0, UNITS // 2 - 1) as i:
                unit(2 * i + 1, 1)
                unit(2 * i + 2, 0)
            unit(7, 1, nxt=False)
            m = UNITS - 1
            add_logits(m, 1, 4)
            softmax(m)
            band_low(m)
            outputs(m, 1, 0)
            outputs(m, 1, 1)

            def last_centre(i):
                dve.wait_ge(q_mean, i + 1)
                for h in range(HALVES):
                    nc.vector.tensor_tensor(quarter(o, i, h), quarter(o, i, h), ms[:, i % 2, :],
                                            ALU.subtract).then_inc(q_centred, 1)

            def last_normalise(i):
                dve.wait_ge(q_rstd, i + 1)
                dve.wait_ge(q_squared, 2 * i + 2)
                for h in range(HALVES):
                    dve.wait_ge(q_centred, 2 * i + h + 1)
                    nc.vector.tensor_tensor(quarter(o, i, h), quarter(o, i, h),
                                            rs[:, (i % 2) * BANK:(i % 2 + 1) * BANK], ALU.mult).then_inc(q_normed, 1)
                dve.wait_ge(s_norm_in, 64)
                dve.wait_ge(q_normed, 2 * i + 2)
                nc.vector.tensor_scalar(quarter(o, i, 1), quarter(o, i, 1), lnw[:, 1:2], lnb[:, 1:2], ALU.mult,
                                        ALU.add).then_inc(q_done[1], 1)

            last_centre(0)
            last_centre(1)
            last_centre(2)
            last_normalise(0)
            last_centre(3)
            last_normalise(1)
            last_normalise(2)
            last_normalise(3)


_INS = ["x", "L0_conv_w1", "L0_conv_b1", "L0_conv_w2", "L0_conv_b2", "L1_conv_A", "L1_conv_Bvec", "L1_conv_Cmat",
        "L1_conv_D", "L1_conv_ln_w", "L1_conv_ln_b"]
_OUT = (BATCH, CH, HEIGHT, WIDTH)


def kernel(**inputs):
    import numpy as _np
    import concourse.bacc as _bacc
    from concourse.bass_utils import run_bass_kernel_spmd as _run

    nc = _bacc.Bacc("TRN2", target_bir_lowering=False, num_devices=1)
    arrays, args = {}, []
    for name in _INS:
        a = _np.ascontiguousarray(inputs[name])
        arrays[f"in_{name}_dram"] = a
        args.append(nc.dram_tensor(f"in_{name}_dram", a.shape, mybir.dt.from_np(a.dtype), kind="ExternalInput").ap())
    args.append(nc.dram_tensor("out_0_dram", _OUT, F32, kind="ExternalOutput").ap())
    conv_seq_kernel(nc, *args)
    r = _run(nc, [arrays], core_ids=[0])
    return r.results[0]["out_0_dram"]
```

```python
from contextlib import ExitStack

import concourse.bass as bass
from concourse import mybir

F32 = mybir.dt.float32
F16 = mybir.dt.float16
U32 = mybir.dt.uint32
ALU = mybir.AluOpType
ACT = mybir.ActivationFunctionType
AX = mybir.AxisListType.X
ABSMAX = bass.bass_isa.ReduceOp.absmax

P = 128
BATCH, CH, HEIGHT, WIDTH = 4, 256, 64, 64
HALVES = CH // P
MID = 128
K7 = 7
TAPS = K7 * K7
ROWS, COLS = HEIGHT // 2, WIDTH // 2
PAD = 3
PROWS = ROWS + 2 * PAD
V_ORDER = (3, 0, 1, 2, 4, 5, 6)
TILE_ROWS = ROWS // 2
VROWS = TILE_ROWS + 2
UNITS = BATCH * 2
TILES = 2 * (ROWS // 4)
BROWS = 4 + 2 * PAD
BANK = 512
LO = 64
STATE = 32
LN_EPS = 1e-5
SEL_TAPS = ((0, 7), (3, 7), (2, 7), (1, 7), (0, 6), (0, 5), (0, 4))
SEL_AT = PAD * COLS + COLS - 1 - PAD
ATT_SCALE = 4096.0
COMPS = 9
STREAMS = COMPS * K7
GROUP = (0, 0, 1, 1, 2, 2, 3, 3, 4)
GROUP_END = (2, 4, 6, 8, 9)
COMP_STEPS = HALVES * K7
CONV_STEPS = COMPS * COMP_STEPS
RING = 3
SOURCE_ROW = (2, 0, 2, 1, 2, 0, 2, 0, 0)
T_STEP = (0, 1, None, 2, 3, 4, 5, 6, None)
X_SCALE = 2.0 ** 12
QUARTERS = 4
SCAN_STEPS = 6
TURN_X = 92
MEAN_0, VARIANCE_0, MEAN_1, VARIANCE_1 = 58, 69, 73, 84


def conv_seq_kernel(nc, x, w1, b1, w2, b2, A, Bvec, Cmat, D, ln_w, ln_b, out):
    with ExitStack() as ctx:
        def sb(name, shape, dt=F32):
            return ctx.enter_context(nc.sbuf_tensor(name, shape, dt))

        def sem(name):
            return ctx.enter_context(nc.semaphore(name))

        xv = x.rearrange("b (h p) (r e) w -> b e h p r w", p=P, e=2)
        ov = out.rearrange("b (h p) (r e) w -> b e h p r w", p=P, e=2)

        id32 = sb("id32", [P, P])
        id16 = sb("id16", [P, P], F16)
        sel = sb("sel", [P, len(SEL_TAPS), (BROWS + 4) * COLS], F16)
        ones = sb("ones", [P, P])
        eps = sb("eps", [P, 1])
        W = sb("W", [P, 2, HALVES, STREAMS, TAPS], F16)
        bias = sb("bias", [P, 1])
        winv = sb("winv", [P, 1])
        yc = sb("yc", [P, HALVES, WIDTH])
        dcol = sb("dcol", [P, HALVES])
        lnw = sb("lnw", [P, HALVES])
        lnb = sb("lnb", [P, HALVES])
        raw = sb("raw", [P, 2, HALVES, PROWS, WIDTH])
        V = sb("V", [P, RING, 2, HALVES, 2, TILE_ROWS, COLS], F16)
        raw_in = [sem("raw_in_even"), sem("raw_in_odd")]
        first_in = [sem("first_in_0"), sem("first_in_1")]
        T = sb("T", [P, HALVES, VROWS, WIDTH])
        A_rows = sb("A_rows", [P, HALVES, VROWS, WIDTH])
        Z = sb("Z", [P, TILE_ROWS, 2, COLS])
        amx = sb("amx", [P, 2, HALVES])
        aall = sb("aall", [P, 2, HALVES])
        sc = sb("sc", [P, 2, 10])

        with ExitStack() as early:
            def tmp(name, shape, dt=F32):
                return early.enter_context(nc.sbuf_tensor(name, shape, dt))

            def ptmp(name, shape):
                return early.enter_context(nc.psum_tensor(name, shape, F32))

            w1raw = tmp("w1raw", [P, HALVES, P * TAPS])
            wc = tmp("wc", [P, HALVES, K7, K7 * TAPS])
            ut = tmp("ut", [P, HALVES, 5, K7 * TAPS])
            w2raw = tmp("w2raw", [TAPS, MID])
            w2t = tmp("w2t", [MID, MID])
            b1col = tmp("b1col", [MID, 1])
            b2col = tmp("b2col", [P, 1])
            wmax = tmp("wmax", [P, HALVES * K7 + 1])
            wall = tmp("wall", [P, 1])
            wsc = tmp("wsc", [P, 8])
            powA = tmp("powA", [STATE, 2, 2, STATE])
            states = tmp("states", [STATE, WIDTH])
            cm = tmp("cm", [STATE, CH])
            pst = ptmp("pst", [P, 2, BANK])
            pcomp = ptmp("pcomp", [P, 3, 2 * BANK])

        HL = sb("HL", [P, 16, P], F16)
        AT = sb("AT", [P, 2, ROWS + 12, COLS], F16)
        E = sb("E", [P, 16, TAPS])
        st = sb("st", [P, 4, 16])
        XT = sb("XT", [P, 2, TILES, HALVES, P], F16)
        band = sb("band", [P, 2, TILES, BROWS, COLS], F16)
        tg = sb("tg", [P, HALVES, 16, WIDTH])
        o = sb("o", [P, 2, HALVES, 16, WIDTH])
        chs = sb("chs", [P, 2 * BANK])
        rs = sb("rs", [P, 2 * BANK])

        ms = ctx.enter_context(nc.psum_tensor("ms", [P, 2, BANK], F32))
        cv = ctx.enter_context(nc.psum_tensor("cv", [P, 2, BANK], F32))
        wk = ctx.enter_context(nc.psum_tensor("wk", [P, 4, BANK], F32))
        ms16 = ms[:].bitcast(F16)

        s_w1 = [sem("w1_in_0"), sem("w1_in_1")]
        s_w2, s_scan_in, s_d_in = sem("w2_in"), sem("scan_in"), sem("d_in")
        s_bias_in, s_norm_in = sem("biases_in"), sem("norm_in")
        s_ident, s_sel, s_const, s_border = sem("ident_set"), sem("select_set"), sem("constants_set"), sem("borders_set")
        s_b2z, s_w2z = sem("b2_cleared"), sem("w2t_cleared")
        s_w2t, s_w2s = sem("w2_turned"), sem("w2t_copied")
        s_comp, s_wcp, s_wmax, s_wall = sem("composite_ready"), sem("composite_copied"), sem("wmax_steps"), sem("wmax_all")
        s_wscale, s_u = sem("wscale_steps"), sem("row_sum_steps")
        w_high, w_low = sem("w_high"), sem("w_low")
        s_bsum, s_bias = sem("bias_summed"), sem("bias_steps")
        s_at, s_pow, s_powc = sem("a_turned"), sem("powers_ready"), sem("powers_copied")
        s_yc, s_ycc = sem("yc_ready"), sem("yc_copied")
        late_cleared = sem("late_cleared")

        cv_zeroed = sem("cv_zeroed")
        amax_part, amax_all, scale_steps = sem("amax_part"), sem("amax_all"), sem("scale_steps")
        a_made, e_again = sem("a_rows_made"), sem("e_rows_again")
        tsum, vhi, vlo = sem("transform_sum"), sem("v_high"), sem("v_low")
        conv_done, z_evac = sem("component_convolved"), sem("logits_added")
        lt_ready, soft, exp_done = sem("logits_turned"), sem("softmax_steps"), sem("exp_done")
        hl_hi, ht_ready, at_copy = sem("att_high"), sem("att_turned"), sem("att_copied")
        sel_done, bhi, blo = sem("band_spread"), sem("band_high"), sem("band_low")
        y_done, t_made, gelu_done, o_made = sem("y_done"), sem("t_made"), sem("gelu_done"), sem("o_made")
        os_made, mean_done, d_made = sem("os_made"), sem("mean_done"), sem("centred")
        sq_made, ss_made, var_done = sem("squared"), sem("ss_made"), sem("var_done")
        ln_done, rstd, normed, affine = sem("ln_done"), sem("rstd"), sem("normed"), sem("affine_done")
        out_dma = sem("out_dma")
        q_sum = sem("q_sum")
        q_mean, q_centred, q_squared, q_var = sem("q_mean"), sem("q_centred"), sem("q_squared"), sem("q_var")
        q_ln, q_rstd, q_normed, q_done = sem("q_ln"), sem("q_rstd"), sem("q_normed"), [sem("q_done_0"), sem("q_done_1")]
        xt_done, xt_high, xt_low = sem("x_turned"), sem("x_turned_high"), sem("x_turned_low")

        WEIGHT_SOURCE = (("wc", 4, 3), ("wc", 0, 4), ("wc", 6, 3), ("wc", 3, 3), ("ut", 0, 4), ("ut", 1, 6),
                         ("ut", 2, 4), ("ut", 3, 7), ("ut", 4, 5))

        def weight_parts():
            for c, (which, i, scale) in enumerate(WEIGHT_SOURCE):
                for h in range(HALVES):
                    yield h, c, (wc if which == "wc" else ut)[:, h, i, :], scale

        def weight_set(low, h, c):
            return W[:, low, h, c * K7:(c + 1) * K7, :].rearrange("p v k -> p (v k)")

        def component(c, h):
            rows = T if T_STEP[c] is not None else A_rows
            return rows[:, h, SOURCE_ROW[c]:SOURCE_ROW[c] + TILE_ROWS, :].rearrange("p r (c w) -> p w r c", w=2)

        def component_made(n, c, h):
            return (a_made, 2 * n + h + 1) if T_STEP[c] is None else (tsum, 14 * n + 2 * T_STEP[c] + h + 1)

        quarter = lambda t, i, h: t[:, i // 2, h, 8 * (i % 2):8 * (i % 2) + 8, :].rearrange("p r w -> p (r w)")
        square_of = lambda i, h: (T, A_rows)[i // 2][:, h, 8 * (i % 2):8 * (i % 2) + 8, :].rearrange("p r w -> p (r w)")
        column = lambda a: a.rearrange("(p o) -> p o", o=1)
        block = ctx.enter_context(nc.Block())

        @block.sync
        def _(sp):
            def unit(n, par, load=True, tail=True, first=False, b_load=None, b_out=None):
                if load:
                    if not first:
                        sp.wait_ge(tsum, 14 * n)
                        sp.wait_ge(xt_done, 8 * n)
                    for h in range(HALVES):
                        sp.dma_start(raw[:, 1 - par, h, PAD:PAD + ROWS, :],
                                     xv[b_load, 1 - par, h]).then_inc(raw_in[1 - par], 16)
                if tail:
                    for q in range(2):
                        for h in range(HALVES):
                            sp.wait_ge(affine, 4 * (n - 1) + 2 * q + h + 1)
                            sp.dma_start(ov[b_out, 1 - par, h, :, 16 * q:16 * q + 16, :], o[:, q, h]).then_inc(out_dma, 16)

            sp.dma_start(w2raw[:, :], w2.rearrange("k m a b -> k (m a b)")).then_inc(s_w2, 16)
            for h in range(HALVES):
                sp.dma_start(w1raw[:, h, :],
                             w1.rearrange("m (h c) a b -> h m (c a b)", h=HALVES)[h]).then_inc(s_w1[h], 16)
                sp.dma_start(raw[:, 0, h, PAD:PAD + ROWS, :], xv[0, 0, h]).then_inc(first_in[h], 16)
            unit(0, 0, tail=False, first=True, b_load=0)
            for n in range(1, UNITS - 1):
                unit(n, n % 2, b_load=(n + 1) // 2, b_out=(n - 1) // 2)
            unit(7, 1, load=False, b_out=3)
            for i in range(QUARTERS):
                for h in range(HALVES):
                    sp.wait_ge(q_done[h], i + 1)
                    sp.dma_start(ov[BATCH - 1, 1, h, :, 8 * i:8 * i + 8, :],
                                 o[:, i // 2, h, 8 * (i % 2):8 * (i % 2) + 8, :]).then_inc(out_dma, 16)
            sp.wait_ge(out_dma, 64 * (UNITS - 1) + 16 * HALVES * QUARTERS)

        @block.gpsimd
        def _(pool):
            def amax(n, par):
                pool.wait_ge(amax_part, 2 * n + 2)
                nc.gpsimd.partition_all_reduce(aall[:, par, :], amx[:, par, :], P, ABSMAX).then_inc(amax_all, 1)

            def unit(n, par, tail=True, prep=True):
                if tail:
                    m = n - 1
                    for q in range(2):
                        pool.wait_ge(o_made, 8 * m + 4 * q + 4)
                        if q:
                            pool.wait_ge(var_done, 2 * m + 1)
                        nc.gpsimd.tensor_tensor(chs[:, :], o[:, q, 0].rearrange("p r w -> p (r w)"),
                                                o[:, q, 1].rearrange("p r w -> p (r w)"), ALU.add).then_inc(os_made, 1)
                        pool.wait_ge(sq_made, 4 * m + 2 * q + 2)
                        pool.wait_ge(mean_done, 2 * m + q + 1)
                        nc.gpsimd.tensor_tensor(chs[:, :], tg[:, 0].rearrange("p r w -> p (r w)"),
                                                tg[:, 1].rearrange("p r w -> p (r w)"), ALU.add).then_inc(ss_made, 1)
                if prep:
                    amax(n + 1, 1 - par)
                if tail:
                    pool.wait_ge(var_done, 2 * n)

            def constants():
                for n, t in enumerate((id32, id16)):
                    nc.gpsimd.memset(t[:, :], 0.0).then_inc(s_ident, 1)
                    pool.wait_ge(s_ident, 2 * n + 1)
                    nc.gpsimd.affine_select(out=t[:, :], in_=t[:, :], compare_op=ALU.not_equal, fill=1.0, base=0,
                                            pattern=[[-1, P]], channel_multiplier=1).then_inc(s_ident, 1)
                nc.gpsimd.memset(ones[:, :], 1.0 / CH).then_inc(s_const, 1)
                nc.gpsimd.memset(eps[:, :], LN_EPS).then_inc(s_const, 1)
                for slot in range(2):
                    for r in (0, PAD + ROWS):
                        nc.gpsimd.memset(raw[:, slot, :, r:r + PAD, :], 0.0).then_inc(s_border, 1)
                nc.gpsimd.memset(sel[:, :, :], 0.0).then_inc(s_sel, 1)
                for n, base in enumerate((0, -LO)):
                    pool.wait_ge(s_sel, 7 * n + 1)
                    for s, (v0, v1) in enumerate(SEL_TAPS):
                        v = sel[:, s, SEL_AT:SEL_AT + K7 * COLS].rearrange("p (u c) -> p u c", u=K7)[:, :, v0:v1]
                        nc.gpsimd.affine_select(out=v, in_=v, compare_op=ALU.not_equal, fill=1.0, base=base - v0,
                                                pattern=[[-K7, K7], [-1, v1 - v0]],
                                                channel_multiplier=1).then_inc(s_sel, 1)

            constants()
            amax(0, 0)
            pool.wait_ge(s_wmax, HALVES * K7 + 1)
            nc.gpsimd.partition_all_reduce(wall[:, :], wmax[:, HALVES * K7:], P, ABSMAX).then_inc(s_wall, 1)
            unit(0, 0, tail=False)
            for n in range(1, UNITS - 1):
                unit(n, n % 2)
            unit(7, 1, prep=False)
            for i in range(2):
                pool.wait_ge(o_made, 8 * (UNITS - 1) + 4)
                nc.gpsimd.tensor_tensor(chs[:, i * BANK:(i + 1) * BANK], quarter(o, i, 0), quarter(o, i, 1),
                                        ALU.add).then_inc(q_sum, 1)

        @block.tensor
        def _(pe):
            def conv(n, par, first, last, warm=True):
                for step in range(first, last):
                    c, h, v = step // COMP_STEPS, step // K7 % HALVES, V_ORDER[step % K7]
                    c0, c1 = max(0, PAD - v), min(COLS, COLS + PAD - v)
                    g = GROUP[c]
                    group_first, group_last = c == 0 or GROUP[c - 1] != g, c + 1 == GROUP_END[g]
                    if step % COMP_STEPS == 0:
                        if group_first and (warm or g >= 2):
                            pe.wait_ge(z_evac, 8 * n + (-2, 0, 1, 2, 4)[g])
                        if not warm:
                            pe.wait_ge(w_low, 2 * c + 2)
                    if step % K7 == 0:
                        pe.wait_ge(vlo, 18 * n + 2 * c + h + 1)
                    for k, (wl, xl) in enumerate(((0, 0), (0, 1), (1, 0))):
                        for w in range(2):
                            bank = cv[LO * w:LO * w + TAPS, (par + g) % 2, :].rearrange("p (r c) -> p r c", c=COLS)
                            ins = pe.matmul(bank[:, :, c0:c1], W[:, wl, h, c * K7 + v, :],
                                            V[:, c % RING, xl, h, w, :, c0 + v - PAD:c1 + v - PAD],
                                            skip_group_check=True,
                                            start=(group_first and step % COMP_STEPS == 0 and k == 0),
                                            stop=(group_last and step % COMP_STEPS == COMP_STEPS - 1 and k == 2))
                    if step % COMP_STEPS == COMP_STEPS - 1:
                        ins.then_inc(conv_done, 1)

            def turn_logits(m):
                pe.wait_ge(z_evac, 8 * m + 8)
                for t in range(8):
                    ins = pe.transpose(ms[:, t // 4, (t % 4) * P:(t % 4 + 1) * P],
                                       Z[:, 2 * t:2 * t + 2].rearrange("p a e c -> p (a e c)"), id32[:, :])
                ins.then_inc(lt_ready, 1)

            def turn_attention(m, g):
                pe.wait_ge(soft, 7 * m + 7)
                for t in range(4):
                    for w in range(2):
                        c = w * 4 * P + t * P
                        ins = pe.transpose(ms16[:, g, c:c + P], HL[:, (4 * g + t) * 2 + w, :], id16[:, :])
                ins.then_inc(ht_ready, 1)

            def spread(m, r):
                if r == 0:
                    pe.wait_ge(at_copy, 2 * m + 2)
                    pe.wait_ge(xt_low, 8 * m + 8)
                if r >= 4:
                    pe.wait_ge(blo, 10 * m + r - 3)
                for c in range(COLS):
                    s = c + 1 if c < PAD else c - COLS + 7 if c >= COLS - PAD else 0
                    f = (BROWS - 1 - r) * COLS + COLS - 1 - c
                    ins = pe.matmul(wk[:, r % 4, c * TILES:(c + 1) * TILES].rearrange("p (w j) -> p w j", w=2),
                                    sel[:, s, f:f + P],
                                    AT[:, :, r:r + 29:4, c], start=True, stop=True)
                ins.then_inc(sel_done, 1)

            def apply(m, y):
                q, h, w = y // 4, y // 2 % 2, y % 2
                if y == 0:
                    pe.wait_ge(blo, 10 * m + 10)
                if y >= 4:
                    pe.wait_ge(o_made, 8 * m + y - 3)
                begin = True
                for j in range(ROWS // 4):
                    r0, r1 = max(4 * j - PAD, 16 * q), min(4 * j + 4 + PAD, 16 * q + 16)
                    if r0 >= r1:
                        continue
                    for k, (xl, bl) in enumerate(((0, 0), (1, 0), (0, 1))):
                        ins = pe.matmul(wk[:, y % 4, (r0 - 16 * q) * COLS:(r1 - 16 * q) * COLS],
                                        XT[:, xl, 8 * w + j, h, :],
                                        band[:, bl, 8 * w + j, r0 - 4 * j + PAD:r1 - 4 * j + PAD, :]
                                        .rearrange("p r c -> p (r c)"),
                                        start=begin, stop=(k == 2 and r1 == 16 * q + 16 and 4 * j + 4 - PAD >= 16 * q + 13),
                                        skip_group_check=True)
                        begin = False
                ins.then_inc(y_done, 1)

            def mean(m, q):
                pe.wait_ge(os_made, 2 * m + q + 1)
                if q:
                    pe.wait_ge(ln_done, 2 * m + 1)
                for e in range(2):
                    ins = pe.matmul(ms[:, e, :], ones[:, :], chs[:, e * BANK:(e + 1) * BANK], start=True, stop=True)
                ins.then_inc(mean_done, 1)

            def variance(m, q):
                pe.wait_ge(ss_made, 2 * m + q + 1)
                pe.wait_ge(d_made, 4 * m + 2 * q + 2)
                for e in range(2):
                    ins = pe.matmul(ms[:, e, :], ones[:, :], chs[:, e * BANK:(e + 1) * BANK], start=True, stop=True)
                ins.then_inc(var_done, 1)

            def turn_x(n, par, g, warm=True):
                if g == 0 and warm:
                    pe.wait_ge(o_made, 8 * n)
                if g >= 4:
                    pe.wait_ge(xt_low, 8 * n + g - 3)
                for t in range(2):
                    for h in range(HALVES):
                        w, j = (2 * g + t) // 8, (2 * g + t) % 8
                        c = (t * HALVES + h) * P
                        rows = raw[:, par, h, PAD + 4 * j:PAD + 4 * j + 4, :].rearrange("p r w -> p (r w)")
                        ins = pe.transpose(wk[:, g % 4, c:c + P], rows[:, w:4 * WIDTH:2], id32[:, :])
                ins.then_inc(xt_done, 1)

            def unit(n, par):
                m = n - 1
                conv(n, par, 0, 3)
                turn_logits(m)
                conv(n, par, 3, 17)
                turn_attention(m, 0)
                turn_attention(m, 1)
                for r in range(BROWS):
                    conv(n, par, (17, 20)[r > 0] + 2 * max(r - 1, 0), 20 + 2 * r)
                    spread(m, r)
                for y in range(8):
                    conv(n, par, (38, 42)[y > 0] + 2 * max(y - 1, 0), 42 + 2 * y)
                    apply(m, y)
                conv(n, par, 56, MEAN_0)
                mean(m, 0)
                conv(n, par, MEAN_0, VARIANCE_0)
                variance(m, 0)
                conv(n, par, VARIANCE_0, MEAN_1)
                mean(m, 1)
                conv(n, par, MEAN_1, VARIANCE_1)
                variance(m, 1)
                conv(n, par, VARIANCE_1, TURN_X)
                for g in range(8):
                    conv(n, par, TURN_X + 2 * max(g - 1, 0), TURN_X + 2 * g)
                    turn_x(n, par, g)
                conv(n, par, TURN_X + 14, CONV_STEPS)
                pe.wait_ge(ln_done, 2 * n)

            def scan_step(j):
                n = 1 << j
                pe.wait_ge(s_powc, 3 * j + 1)
                pe.matmul(pst[0:STATE, 0, 0:n], powA[:, j % 2, 1, :], states[:, 0:n], start=True, stop=True)
                pe.matmul(pst[0:STATE, 0, 64:96], powA[:, j % 2, 1, :], powA[:, j % 2, 0, :], start=True, stop=True)
                pe.matmul(pst[0:STATE, 0, 128:160], powA[:, j % 2, 0, :], powA[:, j % 2, 1, :],
                          start=True, stop=True).then_inc(s_pow, 1)

            def composite(g):
                h, u = g // K7, g % K7
                if u == 0:
                    pe.wait_ge(s_w1[h], 16)
                if g >= 3:
                    pe.wait_ge(s_wcp, g - 2)
                w1h = w1raw[:, h, :].rearrange("m (c t) -> m t c", t=TAPS)
                for v in range(K7):
                    last = pe.matmul(pcomp[:, g % 3, v * P:(v + 1) * P], w1h[:, u * K7 + v, :], w2t[:, :],
                                     start=True, stop=True)
                last.then_inc(s_comp, 1)

            pe.wait_ge(s_ident, 2)
            pe.wait_ge(s_w2, 16)
            pe.transpose(pst[:, 1, 0:TAPS], w2raw[:, :], id32[0:TAPS, 0:TAPS]).then_inc(s_w2t, 1)
            pe.wait_ge(s_w2s, 1)
            for g in range(K7):
                composite(g)
            pe.wait_ge(s_scan_in, 48)
            pe.transpose(pst[0:STATE, 0, 0:STATE], powA[:, 0, 0, :], id32[0:STATE, 0:STATE]).then_inc(s_at, 1)
            for g in range(K7, 2 * K7):
                composite(g)
                if g - K7 < SCAN_STEPS:
                    scan_step(g - K7)
            pe.wait_ge(s_powc, 3 * SCAN_STEPS + 1)
            for h in range(HALVES):
                last = pe.matmul(pst[:, 0, h * WIDTH:(h + 1) * WIDTH], cm[:, h * P:(h + 1) * P], states[:, :],
                                 start=True, stop=True)
            last.then_inc(s_yc, 1)
            pe.wait_ge(s_border, 4)
            pe.wait_ge(cv_zeroed, 1)
            conv(0, 0, 0, COMP_STEPS, warm=False)
            pe.wait_ge(s_bias_in, 48)
            pe.matmul(pst[0:TAPS, 1, 0:1], w2t[:, 0:TAPS], b1col[:, :], start=True, stop=True)
            pe.matmul(pst[LO:LO + TAPS, 1, 0:1], w2t[:, 0:TAPS], b1col[:, :], start=True, stop=True).then_inc(s_bsum, 1)
            conv(0, 0, COMP_STEPS, 84, warm=False)
            pe.wait_ge(w_low, 2 * COMPS)
            for g in range(8):
                turn_x(0, 0, g, warm=False)
            conv(0, 0, 84, CONV_STEPS, warm=False)
            pe.wait_ge(s_sel, 15)
            pe.wait_ge(s_const, 2)
            with nc.tensor.Fori(0, UNITS // 2 - 1) as i:
                unit(2 * i + 1, 1)
                unit(2 * i + 2, 0)
            unit(UNITS - 1, 1)
            m = UNITS - 1
            turn_logits(m)
            turn_attention(m, 0)
            turn_attention(m, 1)
            for r in range(BROWS):
                spread(m, r)
            def last_mean(i):
                if i < 2:
                    pe.wait_ge(q_sum, i + 1)
                    parts = [chs[:, i * BANK:(i + 1) * BANK]]
                else:
                    pe.wait_ge(o_made, 8 * m + 8)
                    pe.wait_ge(q_centred, 2 * (i - 2) + 2)
                    parts = [quarter(o, i, h) for h in range(HALVES)]
                for k, part in enumerate(parts):
                    ins = pe.matmul(ms[:, i % 2, :], ones[:, :], part, start=(k == 0), stop=(k == len(parts) - 1))
                ins.then_inc(q_mean, 1)

            def last_variance(i):
                pe.wait_ge(q_squared, 2 * i + 2)
                if i >= 2:
                    pe.wait_ge(q_ln, i - 1)
                for h in range(HALVES):
                    ins = pe.matmul(cv[:, i % 2, :], ones[:, :], square_of(i, h), start=(h == 0), stop=(h == 1))
                ins.then_inc(q_var, 1)

            for y in range(7):
                apply(m, y)
            last_mean(0)
            apply(m, 7)
            last_mean(1)
            last_variance(0)
            last_variance(1)
            last_mean(2)
            last_mean(3)
            last_variance(2)
            last_variance(3)

        @block.scalar
        def _(act):
            def v_high(n, par, c, cold=False):
                if not (cold and c < RING):
                    act.wait_ge(conv_done, 9 * n + c - RING + 1)
                for h in range(HALVES):
                    act.wait_ge(*component_made(n, c, h))
                    nc.scalar.activation(V[:, c % RING, 0, h], component(c, h), ACT.Identity,
                                         scale=sc[:, par, 3:4]).then_inc(vhi, 1)

            def turned_x(n, par, groups=(0, 8)):
                for g in range(*groups):
                    act.wait_ge(xt_done, 8 * n + g + 1)
                    nc.scalar.activation(XT[:, 0, 2 * g:2 * g + 2].rearrange("p t h c -> p (t h c)"), wk[:, g % 4, :],
                                         ACT.Identity, scale=sc[:, par, 3:4]).then_inc(xt_high, 1)

            def softmax(m):
                act.wait_ge(soft, 7 * m + 2)
                nc.scalar.activation(E[:, :, :], E[:, :, :], ACT.Exp).then_inc(exp_done, 1)
                act.wait_ge(soft, 7 * m + 6)
                nc.scalar.copy(HL[:, :, 0:TAPS], E[:, :, :]).then_inc(hl_hi, 1)

            def turned_attention(m):
                for g in range(2):
                    act.wait_ge(ht_ready, 2 * m + g + 1)
                    nc.scalar.copy(AT[:, :, PAD + 16 * g:PAD + 16 * g + 16, :].rearrange("p w r c -> p w (r c)"),
                                   ms16[:, g, :].rearrange("p (w f) -> p w f", w=2)).then_inc(at_copy, 1)

            def band_high(m, rows=(0, BROWS)):
                for r in range(*rows):
                    act.wait_ge(sel_done, 10 * m + r + 1)
                    nc.scalar.copy(band[:, 0, :, r, :],
                                   wk[:, r % 4, :].rearrange("p (c t) -> p t c", t=TILES)).then_inc(bhi, 1)

            def gelus(m, parts=((0, 0), (0, 1), (1, 0), (1, 1))):
                for q, h in parts:
                    act.wait_ge(t_made, 8 * m + 4 * q + 2 * h + 2)
                    nc.scalar.activation(tg[:, h], tg[:, h], ACT.Gelu).then_inc(gelu_done, 1)

            def squares(m, q):
                act.wait_ge(o_made, 8 * m + 8)
                if q:
                    act.wait_ge(ss_made, 2 * m + 1)
                for h in range(HALVES):
                    act.wait_ge(d_made, 4 * m + 2 * q + h + 1)
                    nc.scalar.activation(tg[:, h], o[:, q, h], ACT.Square).then_inc(sq_made, 1)

            def finish(m, q):
                if q == 0:
                    act.preload_act_table_set("natural_log_exp_and_others")
                act.wait_ge(var_done, 2 * m + q + 1)
                nc.scalar.activation(rs[:, :], ms[:].rearrange("p a b -> p (a b)"), ACT.Ln,
                                     bias=eps[:, :]).then_inc(ln_done, 1)
                act.wait_ge(ln_done, 2 * m + q + 1)
                nc.scalar.activation(rs[:, :], rs[:, :], ACT.Exp, scale=-0.5).then_inc(rstd, 1)
                for h in range(HALVES):
                    act.wait_ge(normed, 4 * m + 2 * q + h + 1)
                    nc.scalar.activation(o[:, q, h], o[:, q, h], ACT.Identity, bias=lnb[:, h:h + 1],
                                         scale=lnw[:, h:h + 1]).then_inc(affine, 1)

            def prep(n, par):
                act.wait_ge(scale_steps, 9 * n + 6)
                v_high(n, par, 0)
                v_high(n, par, 1)

            def unit(n, par, nxt=True):
                m = n - 1
                softmax(m)
                v_high(n, par, 2)
                turned_attention(m)
                band_high(m, (0, 6))
                v_high(n, par, 3)
                band_high(m, (6, BROWS))
                v_high(n, par, 4)
                gelus(m)
                squares(m, 0)
                v_high(n, par, 5)
                finish(m, 0)
                squares(m, 1)
                v_high(n, par, 6)
                v_high(n, par, 7)
                finish(m, 1)
                turned_x(n, par, (0, 2))
                v_high(n, par, 8)
                turned_x(n, par, (2, 8))
                if nxt:
                    prep(n + 1, 1 - par)

            def weights_high(first, last):
                for h, c, src, scale in list(weight_parts())[first:last]:
                    nc.scalar.activation(weight_set(0, h, c), src, ACT.Identity,
                                         scale=wsc[:, scale:scale + 1]).then_inc(w_high, 1)

            act.dma_start(powA[:, 0, 0, :], A).then_inc(s_scan_in, 16)
            act.dma_start(states[:, 0:1], column(Bvec)).then_inc(s_scan_in, 16)
            act.dma_start(cm[:, :], Cmat).then_inc(s_scan_in, 16)
            for h in range(HALVES):
                act.dma_start(dcol[:, h:h + 1], column(D[h * P:(h + 1) * P])).then_inc(s_d_in, 16)
            act.dma_start(b1col[:, :], column(b1)).then_inc(s_bias_in, 16)
            act.wait_ge(s_b2z, 1)
            for p0 in (0, LO):
                act.dma_start(b2col[p0:p0 + TAPS, :], column(b2)).then_inc(s_bias_in, 16)
            for dst, src in ((lnw, ln_w), (lnb, ln_b)):
                for h in range(HALVES):
                    act.dma_start(dst[:, h:h + 1], column(src[h * P:(h + 1) * P])).then_inc(s_norm_in, 16)
            for g in range(HALVES * K7):
                act.wait_ge(s_comp, g + 1)
                nc.scalar.copy(wc[:, g // K7, g % K7, :].rearrange("p (v k) -> p v k", v=K7),
                               pcomp[:, g % 3, 0:K7 * P].rearrange("p (v k) -> p v k", v=K7)[:, :, 0:TAPS]
                               ).then_inc(s_wcp, 1)
                if g == 2 * K7 - 2:
                    act.wait_ge(s_w2z, 1)
                    act.wait_ge(s_wcp, g + 1)
                    nc.scalar.copy(cv[:].rearrange("p a b -> p (a b)"),
                                   w2t[:, TAPS:TAPS + 1].broadcast_to([P, 2 * BANK])).then_inc(cv_zeroed, 1)
            act.wait_ge(s_wscale, 9)
            weights_high(0, 2)
            act.wait_ge(scale_steps, 6)
            v_high(0, 0, 0, cold=True)
            weights_high(2, 4)
            v_high(0, 0, 1, cold=True)
            weights_high(4, 6)
            v_high(0, 0, 2, cold=True)
            weights_high(6, 8)
            v_high(0, 0, 3)
            v_high(0, 0, 4)
            act.wait_ge(s_const, 2)
            act.wait_ge(s_norm_in, 64)
            act.wait_ge(s_u, 6)
            weights_high(8, 10)
            v_high(0, 0, 5)
            act.wait_ge(s_u, 20)
            weights_high(10, 18)
            v_high(0, 0, 6)
            act.wait_ge(w_low, 2 * COMPS)
            turned_x(0, 0)
            v_high(0, 0, 7)
            v_high(0, 0, 8)
            prep(1, 1)
            act.wait_ge(late_cleared, 2)
            act.preload_act_table_set("natural_log_exp_and_others")
            with nc.scalar.Fori(0, UNITS // 2 - 1) as i:
                unit(2 * i + 1, 1)
                unit(2 * i + 2, 0)
            unit(7, 1, nxt=False)
            m = UNITS - 1
            softmax(m)
            turned_attention(m)
            band_high(m)

            def last_squares(i):
                for h in range(HALVES):
                    act.wait_ge(q_centred, 2 * i + h + 1)
                    nc.scalar.activation(square_of(i, h), quarter(o, i, h), ACT.Square).then_inc(q_squared, 1)

            def last_rstd(i):
                act.wait_ge(q_var, i + 1)
                if i >= 2:
                    act.wait_ge(q_normed, 2 * (i - 2) + 2)
                r = rs[:, (i % 2) * BANK:(i % 2 + 1) * BANK]
                nc.scalar.activation(r, cv[:, i % 2, :], ACT.Ln, bias=eps[:, :]).then_inc(q_ln, 1)
                act.wait_ge(q_ln, i + 1)
                nc.scalar.activation(r, r, ACT.Exp, scale=-0.5).then_inc(q_rstd, 1)

            def last_affine(i):
                act.wait_ge(q_normed, 2 * i + 1)
                nc.scalar.activation(quarter(o, i, 0), quarter(o, i, 0), ACT.Identity, bias=lnb[:, 0:1],
                                     scale=lnw[:, 0:1]).then_inc(q_done[0], 1)

            gelus(m, ((0, 0), (0, 1), (1, 0)))
            last_squares(0)
            gelus(m, ((1, 1),))
            last_squares(1)
            act.preload_act_table_set("natural_log_exp_and_others")
            last_rstd(0)
            last_rstd(1)
            last_affine(0)
            last_squares(2)
            last_squares(3)
            last_affine(1)
            last_rstd(2)
            last_rstd(3)
            last_affine(2)
            last_affine(3)

        @block.vector
        def _(dve):
            def paired(dst, par, h, r, rows, pair, op):
                return nc.vector.tensor_tensor(dst[:, h, r:r + rows],
                                               *(raw[:, par, h, 2 * r + d:2 * r + d + 2 * rows - 1:2, :] for d in pair), op)

            def a_rows(n, par, cold=False):
                for h in range(HALVES):
                    if not cold:
                        dve.wait_ge(vlo, 18 * n + h - 1)
                    paired(A_rows, par, h, 0, VROWS, (3, 1), ALU.subtract).then_inc(a_made, 1)

            def t_rows(n, par, c, cold=False, halves=range(HALVES)):
                pair, op = {0: ((0, 2), ALU.subtract), 4: ((1, 2), ALU.add), 6: ((2, 1), ALU.subtract)}[c]
                for h in halves:
                    if not cold:
                        dve.wait_ge(vlo, 18 * n + {0: -4, 4: 6, 6: 10}[c] + h + 1)
                    paired(T, par, h, 0, VROWS, pair, op).then_inc(tsum, 1)

            def e_rows_again(n, par):
                for h in range(HALVES):
                    dve.wait_ge(vlo, 18 * n + 2 + h + 1)
                    paired(T, par, h, 1, TILE_ROWS, (0, 2), ALU.subtract).then_inc(e_again, 1)

            def combine(n, c):
                for h in range(HALVES):
                    if c == 3:
                        dve.wait_ge(e_again, 2 * n + h + 1)
                    else:
                        dve.wait_ge(vlo, 18 * n + 2 * (c - 1) + h + 1)
                        dve.wait_ge(tsum, 14 * n + 2 * T_STEP[c - 1] + h + 1)
                    dve.wait_ge(a_made, 2 * n + h + 1)
                    r = SOURCE_ROW[c]
                    t, a = T[:, h, r:r + TILE_ROWS, :], A_rows[:, h, 0:TILE_ROWS, :]
                    if c == 1:
                        ins = nc.vector.scalar_tensor_tensor(out=t, in0=t, scalar=2.0, in1=a, op0=ALU.mult, op1=ALU.add)
                    elif c == 3:
                        ins = nc.vector.scalar_tensor_tensor(out=t, in0=a, scalar=-2.0, in1=t, op0=ALU.mult,
                                                             op1=ALU.subtract)
                    elif c == 5:
                        ins = nc.vector.tensor_tensor(t, a, t, ALU.subtract)
                    else:
                        ins = nc.vector.scalar_tensor_tensor(out=t, in0=t, scalar=-3.0, in1=a, op0=ALU.mult, op1=ALU.add)
                    ins.then_inc(tsum, 1)

            def v_low(n, par, c, halves=range(HALVES)):
                for h in halves:
                    dve.wait_ge(vhi, 18 * n + 2 * c + h + 1)
                    dve.wait_ge(*component_made(n, c, h))
                    nc.vector.scalar_tensor_tensor(
                        out=V[:, c % RING, 1, h], in0=component(c, h),
                        scalar=sc[:, par, 3:4], in1=V[:, c % RING, 0, h],
                        op0=ALU.mult, op1=ALU.subtract).then_inc(vlo, 1)

            def maxima(n, par, h):
                nc.vector.tensor_reduce(amx[:, par, h:h + 1], raw[:, par, h, PAD:PAD + ROWS, :].rearrange("p r w -> p (r w)"),
                                        AX, ALU.max, apply_absolute_value=True).then_inc(amax_part, 1)

            def unit_maxima(n, par):
                dve.wait_ge(raw_in[par], 16 * n + (16 if par else 0))
                for h in range(HALVES):
                    maxima(n, par, h)

            def scales(n, par):
                dve.wait_ge(amax_all, n + 1)
                s = lambda c, k=1: sc[:, par, c:c + k]
                nc.vector.tensor_scalar(s(0), aall[:, par, 0:1], aall[:, par, 1:2], 1e-30, ALU.max,
                                        ALU.max).then_inc(scale_steps, 1)
                dve.wait_ge(scale_steps, 9 * n + 1)
                nc.vector.tensor_scalar(s(1).bitcast(U32), s(0).bitcast(U32), 0x7F800000, None,
                                        ALU.bitwise_and).then_inc(scale_steps, 1)
                dve.wait_ge(scale_steps, 9 * n + 2)
                nc.vector.reciprocal(s(2), s(1)).then_inc(scale_steps, 1)
                nc.vector.tensor_scalar(s(6), s(1), 1 / (X_SCALE * ATT_SCALE), None, ALU.mult).then_inc(scale_steps, 1)
                dve.wait_ge(scale_steps, 9 * n + 4)
                nc.vector.tensor_scalar(s(3), s(2), X_SCALE, None, ALU.mult).then_inc(scale_steps, 1)
                nc.vector.tensor_scalar(s(7, 2), dcol[:, :], s(6), None, ALU.mult).then_inc(scale_steps, 1)
                dve.wait_ge(scale_steps, 9 * n + 6)

            def logit_scales(n, par):
                s = lambda c: sc[:, par, c:c + 1]
                nc.vector.tensor_scalar(s(4), s(1), winv[:, :], 1 / X_SCALE, ALU.mult, ALU.mult).then_inc(scale_steps, 1)
                dve.wait_ge(scale_steps, 9 * n + 7)
                nc.vector.tensor_scalar(s(5), s(4), -1.0, None, ALU.mult).then_inc(scale_steps, 1)
                nc.vector.tensor_scalar(s(9), s(4), 2.0, None, ALU.mult).then_inc(scale_steps, 1)
                dve.wait_ge(scale_steps, 9 * n + 9)

            def turned_x_low(n, par, groups=(0, 8)):
                for g in range(*groups):
                    dve.wait_ge(xt_high, 8 * n + g + 1)
                    low, high = (XT[:, l, 2 * g:2 * g + 2].rearrange("p t h c -> p (t h c)") for l in (1, 0))
                    nc.vector.scalar_tensor_tensor(out=low, in0=wk[:, g % 4, :], scalar=sc[:, par, 3:4], in1=high,
                                                   op0=ALU.mult, op1=ALU.subtract).then_inc(xt_low, 1)

            def add_logits(n, par, g, turned=True):
                dve.wait_ge(conv_done, 9 * n + GROUP_END[g])
                src = cv[:, (par + g) % 2, :].rearrange("p (r c) -> p r c", c=COLS)
                if g < 2:
                    if g == 0 and turned:
                        dve.wait_ge(lt_ready, n)
                    nc.vector.tensor_scalar(Z[:, :, g, :], src, sc[:, par, 4:5], bias[:, :], ALU.mult,
                                            ALU.add).then_inc(z_evac, 1)
                else:
                    dve.wait_ge(z_evac, 8 * n + 2 * g - 2)
                    for e, k in enumerate(((4, 4), (4, 5), (4, 9))[g - 2]):
                        nc.vector.scalar_tensor_tensor(out=Z[:, :, e, :], in0=src, scalar=sc[:, par, k:k + 1],
                                                       in1=Z[:, :, e, :], op0=ALU.mult, op1=ALU.add).then_inc(z_evac, 1)

            def softmax(m):
                dve.wait_ge(lt_ready, m + 1)
                logits = ms[:].rearrange("p b (i k) -> p (b i) k", k=LO)[:, :, 0:TAPS]
                wide = lambda c: st[:, c, :].unsqueeze(2).broadcast_to([P, 16, TAPS])
                nc.vector.tensor_reduce(st[:, 0, :], logits, AX, ALU.max).then_inc(soft, 1)
                dve.wait_ge(soft, 7 * m + 1)
                nc.vector.tensor_tensor(E[:, :, :], logits, wide(0), ALU.subtract).then_inc(soft, 1)
                dve.wait_ge(exp_done, m + 1)
                nc.vector.tensor_reduce(st[:, 1, :], E[:, :, :], AX, ALU.add).then_inc(soft, 1)
                dve.wait_ge(soft, 7 * m + 3)
                nc.vector.reciprocal(st[:, 2, :], st[:, 1, :]).then_inc(soft, 1)
                dve.wait_ge(soft, 7 * m + 4)
                nc.vector.tensor_scalar(st[:, 3, :], st[:, 2, :], ATT_SCALE, None, ALU.mult).then_inc(soft, 1)
                dve.wait_ge(soft, 7 * m + 5)
                nc.vector.tensor_tensor(E[:, :, :], E[:, :, :], wide(3), ALU.mult).then_inc(soft, 1)
                dve.wait_ge(hl_hi, m + 1)
                nc.vector.tensor_tensor(HL[:, :, LO:LO + TAPS], E[:, :, :], HL[:, :, 0:TAPS],
                                        ALU.subtract).then_inc(soft, 1)

            def band_low(m, rows=(0, BROWS)):
                for r in range(*rows):
                    dve.wait_ge(bhi, 10 * m + r + 1)
                    nc.vector.tensor_tensor(band[:, 1, :, r, :], wk[:, r % 4, :].rearrange("p (c t) -> p t c", t=TILES),
                                            band[:, 0, :, r, :], ALU.subtract).then_inc(blo, 1)

            def gelu_args(m, par, q, h):
                for w in range(2):
                    y = 4 * q + 2 * h + w
                    dve.wait_ge(y_done, 8 * m + y + 1)
                    nc.vector.scalar_tensor_tensor(
                        out=tg[:, h, :, w:WIDTH:2], in0=wk[:, y % 4, :].rearrange("p (r c) -> p r c", c=COLS),
                        scalar=sc[:, par, 7 + h:8 + h],
                        in1=yc[:, h, w:WIDTH:2].unsqueeze(1).broadcast_to([P, 16, COLS]),
                        op0=ALU.mult, op1=ALU.add).then_inc(t_made, 1)

            def residual(m, par, q, h):
                dve.wait_ge(gelu_done, 4 * m + 2 * q + h + 1)
                for w in range(2):
                    y = 4 * q + 2 * h + w
                    nc.vector.scalar_tensor_tensor(
                        out=o[:, q, h, :, w:WIDTH:2], in0=wk[:, y % 4, :].rearrange("p (r c) -> p r c", c=COLS),
                        scalar=sc[:, par, 6:7], in1=tg[:, h, :, w:WIDTH:2],
                        op0=ALU.mult, op1=ALU.add).then_inc(o_made, 1)

            def outputs(m, par, q):
                for h in range(HALVES):
                    gelu_args(m, par, q, h)
                for h in range(HALVES):
                    residual(m, par, q, h)
                dve.wait_ge(o_made, 8 * m + 4 * q + 4)

            flat = lambda a: a.rearrange("p r w -> p (r w)")

            def centre(m, q):
                dve.wait_ge(mean_done, 2 * m + q + 1)
                dve.wait_ge(os_made, 2 * m + q + 1)
                for h in range(HALVES):
                    nc.vector.tensor_tensor(flat(o[:, q, h]), flat(o[:, q, h]), ms[:].rearrange("p a b -> p (a b)"),
                                            ALU.subtract).then_inc(d_made, 1)

            def normalise(m, q):
                dve.wait_ge(rstd, 2 * m + q + 1)
                dve.wait_ge(sq_made, 4 * m + 2 * q + 2)
                for h in range(HALVES):
                    dve.wait_ge(d_made, 4 * m + 2 * q + h + 1)
                    nc.vector.tensor_tensor(flat(o[:, q, h]), flat(o[:, q, h]), rs[:, :], ALU.mult).then_inc(normed, 1)

            def unit(n, par, nxt=True):
                m = n - 1
                add_logits(m, 1 - par, 4)
                softmax(m)
                v_low(n, par, 2)
                if nxt:
                    unit_maxima(n + 1, 1 - par)
                band_low(m, (0, 2))
                e_rows_again(n, par)
                band_low(m, (2, 4))
                combine(n, 3)
                band_low(m, (4, 6))
                v_low(n, par, 3)
                band_low(m, (6, BROWS))
                t_rows(n, par, 4)
                add_logits(n, par, 0)
                v_low(n, par, 4)
                outputs(m, 1 - par, 0)
                outputs(m, 1 - par, 1)
                add_logits(n, par, 1)
                centre(m, 0)
                combine(n, 5)
                v_low(n, par, 5)
                normalise(m, 0)
                centre(m, 1)
                t_rows(n, par, 6)
                v_low(n, par, 6)
                combine(n, 7)
                v_low(n, par, 7)
                normalise(m, 1)
                add_logits(n, par, 2)
                turned_x_low(n, par, (0, 2))
                v_low(n, par, 8)
                turned_x_low(n, par, (2, 4))
                if nxt:
                    t_rows(n + 1, 1 - par, 0)
                turned_x_low(n, par, (4, 6))
                if nxt:
                    a_rows(n + 1, 1 - par)
                turned_x_low(n, par, (6, 8))
                if nxt:
                    scales(n + 1, 1 - par)
                    logit_scales(n + 1, 1 - par)
                    v_low(n + 1, 1 - par, 0)
                    combine(n + 1, 1)
                add_logits(n, par, 3)
                if nxt:
                    v_low(n + 1, 1 - par, 1)
                dve.wait_ge(out_dma, 64 * n)
                dve.wait_ge(ss_made, 2 * n)

            def scan_copies(j):
                n = 1 << j
                dve.wait_ge(s_pow, j + 1)
                nc.vector.tensor_scalar(states[:, n:2 * n], pst[0:STATE, 0, 0:n], states[:, n - 1:n], None,
                                        ALU.add).then_inc(s_powc, 1)
                nc.vector.tensor_copy(powA[:, (j + 1) % 2, 0, :], pst[0:STATE, 0, 64:96]).then_inc(s_powc, 1)
                nc.vector.tensor_copy(powA[:, (j + 1) % 2, 1, :], pst[0:STATE, 0, 128:160]).then_inc(s_powc, 1)
                dve.wait_ge(s_powc, 3 * j + 4)

            def composite_max(g):
                h, u = g // K7, g % K7
                dve.wait_ge(s_wcp, g + 1)
                nc.vector.tensor_reduce(wmax[:, g:g + 1], wc[:, h, u, :], AX, ALU.max,
                                        apply_absolute_value=True).then_inc(s_wmax, 1)

            def row_sums(h):
                g = lambda u: wc[:, h, u, :]
                u = lambda i: ut[:, h, i, :]
                nc.vector.tensor_tensor(u(2), g(4), g(6), ALU.add).then_inc(s_u, 1)
                dve.wait_ge(s_u, 3 * h + 1)
                nc.vector.tensor_tensor(u(0), u(2), g(5), ALU.add).then_inc(s_u, 1)
                nc.vector.tensor_tensor(u(2), u(2), g(5), ALU.subtract).then_inc(s_u, 1)

            def more_row_sums(h):
                g = lambda u: wc[:, h, u, :]
                u = lambda i: ut[:, h, i, :]
                done = 3 * HALVES + 7 * h
                nc.vector.tensor_tensor(u(3), g(0), g(2), ALU.add).then_inc(s_u, 1)
                nc.vector.tensor_tensor(u(1), g(1), g(3), ALU.add).then_inc(s_u, 1)
                nc.vector.scalar_tensor_tensor(out=u(4), in0=g(3), scalar=2.0, in1=g(2), op0=ALU.mult,
                                               op1=ALU.add).then_inc(s_u, 1)
                dve.wait_ge(s_u, done + 3)
                nc.vector.scalar_tensor_tensor(out=u(4), in0=u(4), scalar=2.0, in1=g(1), op0=ALU.mult,
                                               op1=ALU.add).then_inc(s_u, 1)
                nc.vector.tensor_tensor(u(1), u(3), u(1), ALU.add).then_inc(s_u, 1)
                dve.wait_ge(s_u, done + 5)
                nc.vector.scalar_tensor_tensor(out=u(3), in0=u(3), scalar=2.0, in1=u(1), op0=ALU.mult,
                                               op1=ALU.subtract).then_inc(s_u, 1)
                nc.vector.scalar_tensor_tensor(out=u(4), in0=u(4), scalar=2.0, in1=g(0), op0=ALU.mult,
                                               op1=ALU.add).then_inc(s_u, 1)

            def weight_scales():
                dve.wait_ge(s_wall, 1)
                nc.vector.tensor_scalar(wsc[:, 0:1], wall[:, :], 1e-30, None, ALU.max).then_inc(s_wscale, 1)
                dve.wait_ge(s_wscale, 1)
                nc.vector.tensor_scalar(wsc[:, 1:2].bitcast(U32), wsc[:, 0:1].bitcast(U32), 0x7F800000, None,
                                        ALU.bitwise_and).then_inc(s_wscale, 1)
                dve.wait_ge(s_wscale, 2)
                nc.vector.reciprocal(wsc[:, 2:3], wsc[:, 1:2]).then_inc(s_wscale, 1)
                nc.vector.tensor_scalar(winv[:, :], wsc[:, 1:2], 2.0 ** -13, None, ALU.mult).then_inc(s_wscale, 1)
                dve.wait_ge(s_wscale, 4)
                nc.vector.tensor_scalar(wsc[:, 3:4], wsc[:, 2:3], 2.0 ** 13, None, ALU.mult).then_inc(s_wscale, 1)
                for column, factor in ((4, 0.5), (5, 1 / 6), (6, -0.5), (7, -1 / 6)):
                    nc.vector.tensor_scalar(wsc[:, column:column + 1], wsc[:, 2:3], 2.0 ** 13 * factor, None,
                                            ALU.mult).then_inc(s_wscale, 1)
                dve.wait_ge(s_wscale, 9)

            def weights_low(first, last):
                for n, (h, c, src, scale) in list(enumerate(weight_parts()))[first:last]:
                    dve.wait_ge(w_high, n + 1)
                    nc.vector.scalar_tensor_tensor(out=weight_set(1, h, c), in0=src, scalar=wsc[:, scale:scale + 1],
                                                   in1=weight_set(0, h, c), op0=ALU.mult,
                                                   op1=ALU.subtract).then_inc(w_low, 1)

            nc.vector.memset(b2col[:, :], 0.0).then_inc(s_b2z, 1)
            nc.vector.memset(w2t[:, :], 0.0).then_inc(s_w2z, 1)
            dve.wait_ge(s_w2z, 1)
            dve.wait_ge(s_w2t, 1)
            nc.vector.tensor_copy(w2t[:, 0:TAPS], pst[:, 1, 0:TAPS]).then_inc(s_w2s, 1)
            for g in range(K7):
                composite_max(g)
                if g == 3:
                    dve.wait_ge(first_in[0], 16)
                    maxima(0, 0, 0)
                if g == 4:
                    dve.wait_ge(s_border, 4)
                    t_rows(0, 0, 0, cold=True, halves=(0,))
            dve.wait_ge(s_at, 1)
            nc.vector.tensor_copy(powA[:, 0, 1, :], pst[0:STATE, 0, 0:STATE]).then_inc(s_powc, 1)
            for g in range(K7, 2 * K7):
                composite_max(g)
                if g - K7 < SCAN_STEPS:
                    scan_copies(g - K7)
                if g == 2 * K7 - 3:
                    dve.wait_ge(first_in[1], 16)
                    maxima(0, 0, 1)
            dve.wait_ge(s_wmax, HALVES * K7)
            nc.vector.tensor_reduce(wmax[:, HALVES * K7:], wmax[:, 0:HALVES * K7], AX, ALU.max).then_inc(s_wmax, 1)
            dve.wait_ge(s_d_in, 32)
            scales(0, 0)
            weight_scales()
            weights_low(0, 2)
            v_low(0, 0, 0, halves=(0,))
            t_rows(0, 0, 0, cold=True, halves=(1,))
            v_low(0, 0, 0, halves=(1,))
            a_rows(0, 0, cold=True)
            combine(0, 1)
            weights_low(2, 4)
            v_low(0, 0, 1)
            weights_low(4, 6)
            v_low(0, 0, 2)
            weights_low(6, 8)
            e_rows_again(0, 0)
            combine(0, 3)
            v_low(0, 0, 3)
            row_sums(0)
            row_sums(1)
            t_rows(0, 0, 4)
            v_low(0, 0, 4)
            weights_low(8, 10)
            logit_scales(0, 0)
            dve.wait_ge(s_bsum, 1)
            nc.vector.tensor_copy(bias[:, :], b2col[:, :]).then_inc(s_bias, 1)
            dve.wait_ge(s_bias, 1)
            for p0 in (0, LO):
                nc.vector.tensor_tensor(bias[p0:p0 + TAPS, :], b2col[p0:p0 + TAPS, :], pst[p0:p0 + TAPS, 1, 0:1],
                                        ALU.add).then_inc(s_bias, 1)
            dve.wait_ge(s_bias, 3)
            add_logits(0, 0, 0, turned=False)
            more_row_sums(0)
            more_row_sums(1)
            combine(0, 5)
            v_low(0, 0, 5)
            weights_low(10, 18)
            add_logits(0, 0, 1)
            t_rows(0, 0, 6)
            v_low(0, 0, 6)
            dve.wait_ge(s_yc, 1)
            nc.vector.tensor_copy(yc[:, :, :], pst[:, 0, 0:HALVES * WIDTH].rearrange(
                "p (h w) -> p h w", h=HALVES)).then_inc(s_ycc, 1)
            dve.wait_ge(w_low, 18)
            dve.wait_ge(s_ycc, 1)
            nc.vector.memset(HL[:].rearrange("p i k -> p (i k)").bitcast(U32), 0).then_inc(late_cleared, 1)
            nc.vector.memset(AT[:].rearrange("p w r c -> p (w r c)").bitcast(U32), 0).then_inc(late_cleared, 1)
            dve.wait_ge(late_cleared, 2)
            turned_x_low(0, 0)
            combine(0, 7)
            v_low(0, 0, 7)
            add_logits(0, 0, 2)
            v_low(0, 0, 8)
            unit_maxima(1, 1)
            scales(1, 1)
            logit_scales(1, 1)
            t_rows(1, 1, 0)
            a_rows(1, 1)
            v_low(1, 1, 0)
            combine(1, 1)
            add_logits(0, 0, 3)
            v_low(1, 1, 1)
            with nc.vector.Fori(0, UNITS // 2 - 1) as i:
                unit(2 * i + 1, 1)
                unit(2 * i + 2, 0)
            unit(7, 1, nxt=False)
            m = UNITS - 1
            add_logits(m, 1, 4)
            softmax(m)
            band_low(m)
            outputs(m, 1, 0)

            def last_centre(i):
                if i < 2:
                    dve.wait_ge(q_sum, i + 1)
                dve.wait_ge(q_mean, i + 1)
                for h in range(HALVES):
                    nc.vector.tensor_tensor(quarter(o, i, h), quarter(o, i, h), ms[:, i % 2, :],
                                            ALU.subtract).then_inc(q_centred, 1)

            def last_normalise(i):
                dve.wait_ge(q_rstd, i + 1)
                dve.wait_ge(q_squared, 2 * i + 2)
                for h in range(HALVES):
                    dve.wait_ge(q_centred, 2 * i + h + 1)
                    nc.vector.tensor_tensor(quarter(o, i, h), quarter(o, i, h),
                                            rs[:, (i % 2) * BANK:(i % 2 + 1) * BANK], ALU.mult).then_inc(q_normed, 1)
                dve.wait_ge(s_norm_in, 64)
                dve.wait_ge(q_normed, 2 * i + 2)
                nc.vector.tensor_scalar(quarter(o, i, 1), quarter(o, i, 1), lnw[:, 1:2], lnb[:, 1:2], ALU.mult,
                                        ALU.add).then_inc(q_done[1], 1)

            gelu_args(m, 1, 1, 0)
            last_centre(0)
            gelu_args(m, 1, 1, 1)
            last_centre(1)
            residual(m, 1, 1, 0)
            residual(m, 1, 1, 1)
            last_normalise(0)
            last_centre(2)
            last_centre(3)
            last_normalise(1)
            last_normalise(2)
            last_normalise(3)


_INS = ["x", "L0_conv_w1", "L0_conv_b1", "L0_conv_w2", "L0_conv_b2", "L1_conv_A", "L1_conv_Bvec", "L1_conv_Cmat",
        "L1_conv_D", "L1_conv_ln_w", "L1_conv_ln_b"]
_OUT = (BATCH, CH, HEIGHT, WIDTH)


def kernel(**inputs):
    import numpy as _np
    import concourse.bacc as _bacc
    from concourse.bass_utils import run_bass_kernel_spmd as _run

    nc = _bacc.Bacc("TRN2", target_bir_lowering=False, num_devices=1)
    arrays, args = {}, []
    for name in _INS:
        a = _np.ascontiguousarray(inputs[name])
        arrays[f"in_{name}_dram"] = a
        args.append(nc.dram_tensor(f"in_{name}_dram", a.shape, mybir.dt.from_np(a.dtype), kind="ExternalInput").ap())
    args.append(nc.dram_tensor("out_0_dram", _OUT, F32, kind="ExternalOutput").ap())
    conv_seq_kernel(nc, *args)
    r = _run(nc, [arrays], core_ids=[0])
    return r.results[0]["out_0_dram"]
```
